# Optimizing a Trainium2 kernel written in Bass

```python
import numpy as np
import jax
import jax.numpy as jnp

def _softmax(x, axis=-1):
    return jax.nn.softmax(x, axis=axis)

def _gelu(x):
    return jax.nn.gelu(x, approximate=True)

def _silu(x):
    return jax.nn.silu(x)

def _sigmoid(x):
    return jax.nn.sigmoid(x)

def _layernorm(x, axis=-1, eps=1e-05):
    m = jnp.mean(x, axis=axis, keepdims=True)
    v = jnp.var(x, axis=axis, keepdims=True)
    return (x - m) / jnp.sqrt(v + eps)

def _scatter_add(tgt, idx, src, axis=0):
    return tgt.at[idx].add(src)

def _segment_sum(src, seg, n):
    return jax.ops.segment_sum(src, seg, n)
kernel_name = 'mk_gnn_resnorm_d2_gnn_r32_5c9825'

def setup_inputs(seed: int=0):
    np.random.seed(seed)
    _w = jnp.asarray

    def _rec_inputs():
        import jax
        import jax.numpy as jnp
        _gk = jax.random.key(seed)
        x = -0.0005963 + 1.001 * jax.random.normal(jax.random.fold_in(_gk, 1), (96, 1024), jnp.float32)
        _s = jax.random.randint(jax.random.fold_in(_gk, 2), (1536,), 0, 96, jnp.int32)
        _d = jax.random.randint(jax.random.fold_in(_gk, 3), (1536,), 0, 96, jnp.int32)
        _loop = jnp.arange(96, dtype=jnp.int32)
        src = jnp.concatenate([_s, _d, _loop])
        dst = jnp.concatenate([_d, _s, _loop])
        _o = jnp.argsort(dst, stable=True)
        src = src[_o]
        dst = dst[_o]
        edge_type_5 = jax.random.randint(jax.random.fold_in(_gk, 13), (3168,), 0, 5, jnp.int32)
        return (x, src, dst, edge_type_5)
    x, src, dst, edge_type_5 = _rec_inputs()

    def _L0_gnn_setup():
        import jax, jax.numpy as jnp
        import numpy as np
        N = 96
        E = 3072
        IN_F = 1024
        OUT_F = 1024
        H = 16
        D = OUT_F // H
        NUM_ETYPES = 4

        def _build_mask(edge_index, edge_type, edge_type_weights, dtype):
            src, dst = (edge_index[0], edge_index[1])
            w = jax.nn.softplus(edge_type_weights)
            mask = jnp.full((N, N), -jnp.inf, dtype=dtype)
            mask = mask.at[src, dst].set(w[edge_type - 1])
            diag = jnp.diagonal(mask)
            idx = jnp.arange(N)
            mask = mask.at[idx, idx].set(jnp.where(jnp.isneginf(diag), w[3], diag))
            return mask
        key = jax.random.key(seed)
        ks = jax.random.split(key, 20)
        p = lambda k, shape: jax.random.normal(k, shape, dtype=jnp.float32) * 0.02
        return {'x': jax.random.normal(ks[0], (N, IN_F), dtype=jnp.float32), 'edge_index': jax.random.randint(ks[1], (2, E), 0, N), 'edge_type': jax.random.randint(ks[2], (E,), 1, NUM_ETYPES + 1), 'edge_type_weights': jnp.ones((NUM_ETYPES,), jnp.float32) + 0.1 * jax.random.normal(ks[3], (NUM_ETYPES,), dtype=jnp.float32), 'wq': p(ks[4], (OUT_F, IN_F)), 'bq': p(ks[5], (OUT_F,)), 'wk': p(ks[6], (OUT_F, IN_F)), 'bk': p(ks[7], (OUT_F,)), 'wv': p(ks[8], (OUT_F, IN_F)), 'bv': p(ks[9], (OUT_F,)), 'wiq': p(ks[10], (OUT_F, OUT_F)), 'biq': p(ks[11], (OUT_F,)), 'wik': p(ks[12], (OUT_F, OUT_F)), 'bik': p(ks[13], (OUT_F,)), 'wiv': p(ks[14], (OUT_F, OUT_F)), 'biv': p(ks[15], (OUT_F,)), 'wo': p(ks[16], (OUT_F, OUT_F)), 'bo': p(ks[17], (OUT_F,))}
    _L0_gnn_all = _L0_gnn_setup()
    _L0_gnn_in = {k: v for k, v in _L0_gnn_all.items() if k in ('edge_type_weights', 'wq', 'bq', 'wk', 'bk', 'wv', 'bv', 'wiq', 'biq', 'wik', 'bik', 'wiv', 'biv', 'wo', 'bo')}
    del _L0_gnn_all

    def _L1_gnn_setup():
        import jax, jax.numpy as jnp
        import numpy as np
        NEG_SLOPE = 0.1
        EPS = 1e-05
        key = jax.random.key(seed)
        k1, k2, k3, k4, k5 = jax.random.split(key, 5)
        N, E, DIN, DOUT = (10000, 5000, 1024, 1024)
        x = jax.random.normal(k1, (N, DIN), dtype=jnp.float32)
        W = jax.random.normal(k2, (DIN, DOUT), dtype=jnp.float32) * 0.02
        a = jax.random.normal(k3, (1, 2 * DOUT), dtype=jnp.float32) * 0.02
        src = jax.random.randint(k4, (E,), 0, N, dtype=jnp.int64)
        dst = jax.random.randint(k5, (E,), 0, N, dtype=jnp.int64)
        return {'x': x, 'W': W, 'a': a, 'src': src, 'dst': dst}
    _L1_gnn_all = _L1_gnn_setup()
    _L1_gnn_in = {k: v for k, v in _L1_gnn_all.items() if k in ('W', 'a')}
    del _L1_gnn_all
    return {'x': x, 'src': src, 'dst': dst, 'edge_type_5': edge_type_5, 'L0_gnn_edge_type_weights': _L0_gnn_in['edge_type_weights'], 'L0_gnn_wq': _L0_gnn_in['wq'], 'L0_gnn_bq': _L0_gnn_in['bq'], 'L0_gnn_wk': _L0_gnn_in['wk'], 'L0_gnn_bk': _L0_gnn_in['bk'], 'L0_gnn_wv': _L0_gnn_in['wv'], 'L0_gnn_bv': _L0_gnn_in['bv'], 'L0_gnn_wiq': _L0_gnn_in['wiq'], 'L0_gnn_biq': _L0_gnn_in['biq'], 'L0_gnn_wik': _L0_gnn_in['wik'], 'L0_gnn_bik': _L0_gnn_in['bik'], 'L0_gnn_wiv': _L0_gnn_in['wiv'], 'L0_gnn_biv': _L0_gnn_in['biv'], 'L0_gnn_wo': _L0_gnn_in['wo'], 'L0_gnn_bo': _L0_gnn_in['bo'], 'L1_gnn_W': _L1_gnn_in['W'], 'L1_gnn_a': _L1_gnn_in['a']}

def reference(x, src, dst, edge_type_5, L0_gnn_edge_type_weights, L0_gnn_wq, L0_gnn_bq, L0_gnn_wk, L0_gnn_bk, L0_gnn_wv, L0_gnn_bv, L0_gnn_wiq, L0_gnn_biq, L0_gnn_wik, L0_gnn_bik, L0_gnn_wiv, L0_gnn_biv, L0_gnn_wo, L0_gnn_bo, L1_gnn_W, L1_gnn_a):
    import jax
    import jax.numpy as jnp

    def _L0_gnn_ref(x, edge_index, edge_type, edge_type_weights, wq, bq, wk, bk, wv, bv, wiq, biq, wik, bik, wiv, biv, wo, bo):
        import jax, jax.numpy as jnp
        import numpy as np
        N = 96
        E = 3072
        IN_F = 1024
        OUT_F = 1024
        H = 16
        D = OUT_F // H
        NUM_ETYPES = 4

        def _build_mask(edge_index, edge_type, edge_type_weights, dtype):
            src, dst = (edge_index[0], edge_index[1])
            w = jax.nn.softplus(edge_type_weights)
            mask = jnp.full((N, N), -jnp.inf, dtype=dtype)
            mask = mask.at[src, dst].set(w[edge_type - 1])
            diag = jnp.diagonal(mask)
            idx = jnp.arange(N)
            mask = mask.at[idx, idx].set(jnp.where(jnp.isneginf(diag), w[3], diag))
            return mask
        q = x @ wq.T + bq
        k = x @ wk.T + bk
        v = x @ wv.T + bv
        q2 = (q @ wiq.T + biq).reshape(N, H, D).transpose(1, 0, 2)
        k2 = (k @ wik.T + bik).reshape(N, H, D).transpose(1, 0, 2)
        v2 = (v @ wiv.T + biv).reshape(N, H, D).transpose(1, 0, 2)
        mask = _build_mask(edge_index, edge_type, edge_type_weights, x.dtype)
        scale = 1.0 / np.sqrt(D).astype(np.float32)
        scores = jnp.einsum('hnd,hmd->hnm', q2, k2) * scale + mask[None]
        attn = jax.nn.softmax(scores, axis=-1)
        out = jnp.einsum('hnm,hmd->hnd', attn, v2)
        out = out.transpose(1, 0, 2).reshape(N, OUT_F)
        return out @ wo.T + bo

    def _L1_gnn_ref(x, W, a, src, dst):
        import jax, jax.numpy as jnp
        import numpy as np
        NEG_SLOPE = 0.1
        EPS = 1e-05
        N = x.shape[0]
        d = W.shape[1]
        h = x @ W
        a_l, a_r = (a[0, :d], a[0, d:])
        al = h @ a_l
        ar = h @ a_r
        e = jnp.exp(-jax.nn.leaky_relu(al[src] + ar[dst], negative_slope=NEG_SLOPE))
        rowsum = jax.ops.segment_sum(e, src, num_segments=N)
        h_prime = jax.ops.segment_sum(e[:, None] * h[dst], src, num_segments=N)
        h_prime = h_prime / (rowsum[:, None] + EPS)
        return jax.nn.elu(h_prime)
    edge_index = jnp.stack([src, dst])
    x = _layernorm(x + _L0_gnn_ref(x, edge_index, edge_type_5, L0_gnn_edge_type_weights, L0_gnn_wq, L0_gnn_bq, L0_gnn_wk, L0_gnn_bk, L0_gnn_wv, L0_gnn_bv, L0_gnn_wiq, L0_gnn_biq, L0_gnn_wik, L0_gnn_bik, L0_gnn_wiv, L0_gnn_biv, L0_gnn_wo, L0_gnn_bo), axis=-1)
    x = _layernorm(x + _L1_gnn_ref(x, L1_gnn_W, L1_gnn_a, src, dst), axis=-1)
    return x

_drawn_inputs = setup_inputs


def setup_inputs(seed=0):
    import zlib

    import numpy as np

    out = dict(_drawn_inputs(seed))
    spreads = {}
    factors = {'L0_gnn_edge_type_weights': 42.054,
     'L0_gnn_wq': 6.761,
     'L0_gnn_bq': 8.0,
     'L0_gnn_wk': 6.74,
     'L0_gnn_bk': 64.0,
     'L0_gnn_bv': 6.031,
     'L0_gnn_wiq': 6.834,
     'L0_gnn_biq': 21.342,
     'L0_gnn_wik': 6.785,
     'L0_gnn_bik': 64.0,
     'L0_gnn_biv': 3.845}
    for name, (base, spread) in spreads.items():
        noise = np.random.default_rng([zlib.crc32(name.encode()), seed]).standard_normal(out[name].shape)
        drawn = base * np.exp(spread * noise) if base else spread * noise
        out[name] = jnp.asarray(drawn.astype(out[name].dtype))
    for name, factor in factors.items():
        out[name] = (out[name] * factor).astype(out[name].dtype)
    return out
```

```python
import concourse.bass as bass
from concourse import mybir
from contextlib import ExitStack


def build(nc, x, src, dst, edge_type_5, etw, wq, bq, wk, bk, wv, bv, wiq, biq, wik, bik, wiv, biv, wo, bo,
          gat_w, gat_a, out):
    f32, bf16, i32 = mybir.dt.float32, mybir.dt.bfloat16, mybir.dt.int32
    ALU, ACT, AX = mybir.AluOpType, mybir.ActivationFunctionType, mybir.AxisListType

    N, F = x.shape
    P = 128
    KC = F // P
    HEADS, HD = 16, F // 16
    HALF = F // 2
    SCALE = HD ** -0.5
    EC = 32
    EP = src.shape[0] // EC
    EG = 4
    NEG = -1.0e30
    EPS = 1e-5

    TR = 256
    TPM = F // TR
    NRAW, NWT = 6, 6
    STREAM = [wq, wk, wiq, wik, wv, wiv, wo]
    TILES = TPM * len(STREAM)
    T_WQ, T_WK, T_WIQ, T_WIK, T_WV, T_WIV, T_WO = [TPM * m for m in range(7)]
    BANDED_OUT = (T_WQ, T_WK, T_WV)
    COLUMNS = (T_WQ, T_WK, T_WIQ, T_WIK, T_WV)

    def matrix_of(tile):
        return tile - tile % TPM

    ctx = ExitStack()
    with ctx:
        def sb(name, shape, dt=f32):
            return ctx.enter_context(nc.sbuf_tensor(name, shape, dt))

        def ps(name):
            return ctx.enter_context(nc.psum_tensor(name, [P, 512], f32))

        def sem(name):
            return ctx.enter_context(nc.semaphore(name))

        raw = sb("raw", [P, NRAW, KC * TR])
        wt = sb("wt", [P, NWT, KC * TR])
        gat_w_sb = sb("gat_w_sb", [P, KC, F])
        x_nodes = sb("x_nodes", [N, F])
        xT = sb("xT", [P, KC, N])
        qT = sb("qT", [P, KC, N])
        kT = sb("kT", [P, KC, N])
        vT = sb("vT", [P, KC, N])
        q2T = sb("q2T", [P, KC, N])
        k2T = sb("k2T", [P, KC, N])
        v2 = sb("v2", [N, F])
        probs = sb("probs", [N, HEADS, N])
        probsT = sb("probsT", [N, HEADS, N])
        mixed = sb("mixed", [N, F])
        y1 = sb("y1", [N, F])
        x1 = sb("x1", [N, F])
        bo_all = sb("bo_all", [N, F])
        gat_a_all = sb("gat_a_all", [N, 2, F])
        ident = sb("ident", [P, P])
        NB = 6
        bias_rows = sb("bias_rows", [NB * KC, P])
        biasT = sb("biasT", [P, NB * KC])
        small = sb("small", [P, 256])
        edge_rows_i = sb("edge_rows_i", [EC, 3, EP], i32)
        edge_rows = sb("edge_rows", [EC, 3, EP])
        edge_rows_b = sb("edge_rows_b", [EC, 2, EP], bf16)
        edge_cols = sb("edge_cols", [EP, 3, EC])
        edge_work = sb("edge_work", [EP, 5, EC])
        times_n = sb("times_n", [EC, EP], bf16)
        times_1 = sb("times_1", [EC, EP], bf16)
        later = sb("later", [EP, EP])
        junk = sb("junk", [P, 512])
        node_ids = sb("node_ids", [EP, N])
        chunk_base = sb("chunk_base", [EP, EC])
        diag3 = sb("diag3", [N, N])
        latest_g = sb("latest_g", [N, EC // EG, N])
        latest = sb("latest", [N, N])
        latest_i = sb("latest_i", [N, N], i32)
        mask = sb("mask", [N, N])
        mask_part = sb("mask_part", [N, N])
        countT = sb("countT", [N, N])
        absentT = sb("absentT", [N, N])
        etw_all = sb("etw_all", [N, 4])
        etw_a = sb("etw_a", [N, 4])
        etw_soft = sb("etw_soft", [N, 4])
        gz = sb("gz", [N, 4, N])
        region = gat_w_sb[:, :, :].rearrange("p k n -> p (k n)").bitcast(bf16)
        key_src = region[0:EC, 0:EC * EP]
        key_dst = region[0:EC, EC * EP:2 * EC * EP]
        at = 2 * EC * EP
        src_hot = region[0:EP, at:at + EC * N].rearrange("p (c n) -> p c n", c=EC)
        dst_hot = region[0:EP, at + EC * N:at + 2 * EC * N].rearrange("p (c n) -> p c n", c=EC)
        dst_val = region[0:EP, at + 2 * EC * N:at + 3 * EC * N].rearrange("p (c n) -> p c n", c=EC)

        x_band = y1
        oT = qT
        x1T = kT
        h = v2
        elu_e = mixed
        elu_r = y1
        x_bo = bo_all
        x1m1 = x_bo
        y2 = probs[:, :, :].rearrange("p h n -> p (h n)")[:, 0:F]
        final = probsT[:, :, :].rearrange("p h n -> p (h n)")[:, 0:F]

        acc = [ps(f"acc{i}") for i in range(2)]
        wide = [ps(f"wide{i}") for i in range(2)]
        misc = [ps(f"misc{i}") for i in range(4)]

        raw_in = [sem(f"raw_in{i}") for i in range(NRAW)]
        x_in, bias_in, edge_in, etw_in = sem("x_in"), sem("bias_in"), sem("edge_in"), sem("etw_in")
        bo_in, gat_a_in, gat_w_in, out_done = sem("bo_in"), sem("gat_a_in"), sem("gat_w_in"), sem("out_done")
        wt_ready, tile_done = sem("wt_ready"), sem("tile_done")
        acc_read, wide_read = sem("acc_read"), sem("wide_read")
        x_band_ready = sem("x_band_ready")
        ident_ready, xT_psum, xT_ready, bias_psum, bias_ready = (
            sem("ident_ready"), sem("xT_psum"), sem("xT_ready"), sem("bias_psum"), sem("bias_ready"))
        pool_const, edge_conv, edge_psum, edge_cols_ready, keys_placed = (
            sem("pool_const"), sem("edge_conv"), sem("edge_psum"), sem("edge_cols_ready"), sem("keys_placed"))
        keys_psum, keys_compared, kept_ready, hot_ready, val_ready = (
            sem("keys_psum"), sem("keys_compared"), sem("kept_ready"), sem("hot_ready"), sem("val_ready"))
        latest_psum, latest_read, count_psum, count_ready = (
            sem("latest_psum"), sem("latest_read"), sem("count_psum"), sem("count_ready"))
        etw_pre, etw_ln, mask_ready = sem("etw_pre"), sem("etw_ln"), sem("mask_ready")
        scores_psum, masked_ready, probs_ready, probsT_psum, probsT_ready = (
            sem("scores_psum"), sem("masked_ready"), sem("probs_ready"), sem("probsT_psum"),
            sem("probsT_ready"))
        mix_psum, mixed_ready, oT_psum, oT_ready = (
            sem("mix_psum"), sem("mixed_ready"), sem("oT_psum"), sem("oT_ready"))
        x_bo_ready, var_ready, rstd_guess, x1_ready, x1T_psum, x1T_ready, x1m1_ready = (
            sem("x_bo_ready"), sem("var_ready"), sem("rstd_guess"), sem("x1_ready"), sem("x1T_psum"),
            sem("x1T_ready"), sem("x1m1_ready"))
        h_psum, h_ready, logits_ready, spread_psum, gexp_in, gexp_out, adj_ready, agg_psum, degree_psum = (
            sem("h_psum"), sem("h_ready"), sem("logits_ready"), sem("spread_psum"), sem("gexp_in"),
            sem("gexp_out"), sem("adj_ready"), sem("agg_psum"), sem("degree_psum"))
        inv_ready, elu_done, final_ready = sem("inv_ready"), sem("elu_done"), sem("final_ready")
        pool_chain, dve_chain, act_chain = sem("pool_chain"), sem("dve_chain"), sem("act_chain")

        STAT, AGG, VEPS, LNV, GUESS, SQ, RSTD, NEGM = 0, 12, 14, 15, 16, 17, 18, 19
        ROWSUM, ROWINV, NMAX, DOTS, AL, INV, ONE = 32, 48, 64, 80, 84, 86, 90

        def col(c, w=1, p=N):
            return small[0:p, c:c + w]

        def bank_of(head):
            return (head % 2) * 2 + head // 8

        def slot_of(head):
            return (head // 2) % 4

        HEADS_OF = [[hh for hh in range(HEADS) if bank_of(hh) == b] for b in range(4)]
        HEAD_ORDER = [hh for b in range(4) for hh in HEADS_OF[b]]

        def quarter(t, n):
            return t[0:N, 0:4 * n].rearrange("p (c n) -> p c n", c=4)

        block = ctx.enter_context(nc.Block())

        @block.sync
        def _(sp):
            def load_tile(tile):
                m, t, slot = matrix_of(tile), tile % TPM, tile % NRAW
                w = STREAM[tile // TPM]
                if m in BANDED_OUT:
                    view = w.rearrange("(c t b) (a i) -> t a b c i", c=8, t=TPM, b=32, a=4)
                else:
                    view = w.rearrange("(t c b) (a i) -> t a b c i", c=8, t=TPM, b=32, a=4)
                if tile >= NRAW:
                    sp.wait_ge(wt_ready, tile - NRAW + 1)
                for a in range(4):
                    sp.dma_start(raw[32 * a:32 * a + 32, slot, :].rearrange("p (c i) -> p c i", c=8),
                                 view[t, a]).then_inc(raw_in[slot], 16)

            sp.dma_start(x_nodes[:, :], x).then_inc(x_in, 16)
            for tile in range(TILES):
                load_tile(tile)
            sp.wait_ge(count_psum, 1)
            sp.wait_ge(val_ready, 1)
            gw = gat_w.rearrange("(k p) n -> p k n", p=P)
            for g in range(4):
                sp.dma_start(gat_w_sb[:, 2 * g:2 * g + 2, :], gw[:, 2 * g:2 * g + 2, :]).then_inc(gat_w_in, 16)
            for half in range(2):
                sp.wait_ge(final_ready, half + 1)
                sp.dma_start(out[:, half * HALF:(half + 1) * HALF],
                             final[:, half * HALF:(half + 1) * HALF]).then_inc(out_done, 16)
            sp.wait_ge(out_done, 32)

        @block.gpsimd
        def _(pool):
            links = [0]

            def link(ins):
                links[0] += 1
                ins.then_inc(pool_chain, 1)
                pool.wait_ge(pool_chain, links[0])

            link(nc.gpsimd.memset(ident[:, :], 0.0))
            nc.gpsimd.affine_select(out=ident[:, :], in_=ident[:, :], compare_op=ALU.not_equal, fill=1.0,
                                    base=0, pattern=[[-1, P]], channel_multiplier=1).then_inc(ident_ready, 1)
            link(nc.gpsimd.memset(later[:, :], 1.0))
            link(nc.gpsimd.memset(diag3[:, :], 0.0))
            nc.gpsimd.memset(small[:, ONE:ONE + 1], 1.0)
            nc.gpsimd.memset(times_n[:, :], float(N))
            nc.gpsimd.memset(times_1[:, :], 1.0)
            nc.gpsimd.iota(node_ids[:, :], pattern=[[1, N]], base=0, channel_multiplier=0,
                           allow_small_or_imprecise_dtypes=True)
            nc.gpsimd.iota(chunk_base[:, :], pattern=[[4, EC]], base=3, channel_multiplier=0,
                           allow_small_or_imprecise_dtypes=True)
            nc.gpsimd.affine_select(out=later[:, :], in_=later[:, :], compare_op=ALU.is_gt, fill=0.0,
                                    base=0, pattern=[[1, EP]], channel_multiplier=-1)
            nc.gpsimd.affine_select(out=diag3[:, :], in_=diag3[:, :], compare_op=ALU.not_equal, fill=3.0,
                                    base=0, pattern=[[-1, N]], channel_multiplier=1).then_inc(pool_const, 1)
            pool.wait_ge(edge_in, 48)
            nc.gpsimd.tensor_copy(edge_rows[:, :, :], edge_rows_i[:, :, :]).then_inc(edge_conv, 1)
            link(nc.gpsimd.tensor_copy(edge_rows_b[:, :, :], edge_rows_i[:, 0:2, :]))
            for k, place in enumerate((key_src, key_dst)):
                nc.gpsimd.affine_select(out=place.rearrange("p (c e) -> p c e", c=EC),
                                        in_=edge_rows_b[:, k:k + 1, :].to_broadcast([EC, EC, EP]),
                                        compare_op=ALU.is_equal, fill=0.0, base=0,
                                        pattern=[[1, EC], [0, EP]], channel_multiplier=-1
                                        ).then_inc(keys_placed, 1)
            pool.wait_ge(edge_cols_ready, 1)
            pool.wait_ge(pool_const, 1)
            for k, hot in enumerate((src_hot, dst_hot)):
                link(nc.gpsimd.tensor_tensor(hot, node_ids[:, :].rearrange("p (c n) -> p c n", c=1)
                                        .to_broadcast([EP, EC, N]),
                                        edge_cols[:, k, :].rearrange("p (c n) -> p c n", n=1)
                                        .to_broadcast([EP, EC, N]), ALU.subtract))
                nc.gpsimd.tensor_scalar(hot, hot, 0.0, None, ALU.is_equal).then_inc(hot_ready, 1)
            pool.wait_ge(hot_ready, 2)
            pool.wait_ge(kept_ready, 1)
            nc.gpsimd.tensor_tensor(dst_val, dst_hot,
                                    edge_work[:, 4, :].rearrange("p (c n) -> p c n", n=1)
                                    .to_broadcast([EP, EC, N]), ALU.mult).then_inc(val_ready, 1)
            pool.wait_ge(x_in, 16)
            pool.wait_ge(bo_in, 16)
            nc.gpsimd.tensor_tensor(x_bo[:, :], x_nodes[:, :], bo_all[:, :], ALU.add).then_inc(x_bo_ready, 1)
            pool.wait_ge(x1_ready, 2)
            nc.gpsimd.tensor_scalar(x1m1[:, :], x1[:, :], -1.0, None, ALU.add).then_inc(x1m1_ready, 1)

        @block.scalar
        def _(act):
            links = [0]

            def link(ins):
                links[0] += 1
                ins.then_inc(act_chain, 1)
                act.wait_ge(act_chain, links[0])

            nc.scalar.preload_act_table_set("natural_log_exp_and_others")
            for k, e in enumerate((src, dst, edge_type_5)):
                act.dma_start(edge_rows_i[:, k, :], e.rearrange("(c e) -> c e", c=EC)).then_inc(edge_in, 16)
            for m, b in enumerate((bq, bk, bv, biv)):
                act.dma_start(bias_rows[KC * m:KC * m + KC, :].rearrange("k (a d) -> k a d", a=4),
                              b.rearrange("(a k d) -> k a d", a=4, k=KC)).then_inc(bias_in, 16)
            for m, b in enumerate((biq, bik)):
                act.dma_start(bias_rows[KC * (4 + m):KC * (5 + m), :],
                              b.rearrange("(k p) -> k p", p=P)).then_inc(bias_in, 16)
            act.dma_start(etw_all[:, :], etw.rearrange("(o n) -> o n", o=1).to_broadcast([N, 4])
                          ).then_inc(etw_in, 16)
            act.dma_start(bo_all[:, :], bo.rearrange("(o n) -> o n", o=1).to_broadcast([N, F])
                          ).then_inc(bo_in, 16)
            act.dma_start(gat_a_all[:, :, :].rearrange("p a n -> p (a n)"), gat_a.to_broadcast([N, 2 * F])
                          ).then_inc(gat_a_in, 16)

            for g in range(2):
                act.wait_ge(xT_psum, g + 1)
                nc.scalar.activation(xT[:, 4 * g:4 * g + 4, :], misc[g][:, 0:4 * N].rearrange(
                    "p (c n) -> p c n", c=4), ACT.Copy).then_inc(xT_ready, 1)
            act.wait_ge(bias_psum, 1)
            nc.scalar.activation(biasT[:, :], misc[2][:, 0:NB * KC], ACT.Copy).then_inc(bias_ready, 1)
            act.wait_ge(etw_pre, 1)
            link(nc.scalar.activation(etw_a[:, :], etw_a[:, :], ACT.Exp))
            nc.scalar.activation(etw_a[:, :], etw_a[:, :], ACT.Ln, bias=1.0).then_inc(etw_ln, 1)
            act.wait_ge(bias_ready, 1)

            dest = {T_WQ: (qT, 0), T_WK: (kT, 1), T_WIQ: (q2T, 4), T_WIK: (k2T, 5), T_WV: (vT, 2)}

            def evacuate(tile, turn):
                act.wait_ge(tile_done, tile + 1)
                m, t = matrix_of(tile), tile % TPM
                to, brow = dest[m]
                for j in range(2):
                    chunk = 4 * j + t if m in BANDED_OUT else 2 * t + j
                    last = nc.scalar.activation(to[:, chunk, :], acc[turn % 2][:, j * N:(j + 1) * N],
                                                ACT.Identity,
                                                bias=biasT[:, KC * brow + chunk:KC * brow + chunk + 1])
                last.then_inc(acc_read, 1)

            def exps(b):
                act.wait_ge(masked_ready, b + 1)
                for hh in HEADS_OF[b]:
                    nc.scalar.activation(probs[:, hh, :], probs[:, hh, :], ACT.Exp,
                                         bias=col(NMAX + 4 * b + slot_of(hh)),
                                         accum_out=col(ROWSUM + hh)).then_inc(probs_ready, 1)

            for tile in range(T_WIV):
                turn = tile
                if tile >= T_WV:
                    exps(tile - T_WV)
                evacuate(tile, turn)
            for b in range(4):
                act.wait_ge(probsT_psum, b + 1)
                nc.scalar.activation(probsT[:, 4 * b:4 * b + 4, :], quarter(misc[b], N), ACT.Copy
                                     ).then_inc(probsT_ready, 1)
            for half in range(2):
                act.wait_ge(tile_done, T_WIV + 2 * half + 2)
                nc.scalar.activation(v2[:, half * HALF:(half + 1) * HALF], wide[half][0:N, :], ACT.Copy
                                     ).then_inc(wide_read, 1)
            act.wait_ge(var_ready, 1)
            link(nc.scalar.activation(col(LNV), col(VEPS), ACT.Ln))
            nc.scalar.activation(col(GUESS), col(LNV), ACT.Exp, scale=-0.5).then_inc(rstd_guess, 1)
            act.wait_ge(x1T_psum, 2)
            nc.scalar.activation(x1T[:, 4:8, :], misc[3][:, 0:4 * N].rearrange("p (c n) -> p c n", c=4),
                                 ACT.Copy).then_inc(x1T_ready, 1)
            for half in range(2):
                act.wait_ge(h_psum, half + 1)
                nc.scalar.activation(h[:, half * HALF:(half + 1) * HALF], acc[half][0:N, :], ACT.Copy
                                     ).then_inc(h_ready, 1)
            act.wait_ge(gexp_in, 1)
            nc.scalar.activation(gz[:, 2, :], gz[:, 1, :], ACT.Exp).then_inc(gexp_out, 1)
            act.wait_ge(inv_ready, 1)
            for half in range(2):
                act.wait_ge(agg_psum, half + 1)
                span = slice(half * HALF, (half + 1) * HALF)
                nc.scalar.activation(elu_e[:, span], wide[half][0:N, :], ACT.Exp, scale=col(INV)
                                     ).then_inc(elu_done, 1)
                nc.scalar.activation(elu_r[:, span], wide[half][0:N, :], ACT.Relu, scale=col(INV)
                                     ).then_inc(elu_done, 1)
            act.wait_ge(var_ready, 2)
            link(nc.scalar.activation(col(LNV), col(VEPS), ACT.Ln))
            nc.scalar.activation(col(GUESS), col(LNV), ACT.Exp, scale=-0.5).then_inc(rstd_guess, 1)

        @block.vector
        def _(dve):
            links = [0]

            def link(ins):
                links[0] += 1
                ins.then_inc(dve_chain, 1)
                dve.wait_ge(dve_chain, links[0])

            def transpose_tile(tile):
                m, slot, to = matrix_of(tile), tile % NRAW, tile % NWT
                dve.wait_ge(raw_in[slot], 64 * (tile // NRAW + 1))
                if tile >= NWT:
                    dve.wait_ge(tile_done, tile - NWT + 1)
                for j in range(2):
                    if m in BANDED_OUT:
                        i = raw[:, slot, :].rearrange("p (A j i) -> p j A i", j=2, i=256)[:, j]
                        o = wt[:, to, :].rearrange("p (k j A b) -> p j A k b", k=KC, j=2, b=32)[:, j]
                    else:
                        i = raw[:, slot, :].rearrange("p (j c i) -> p j c i", j=2, i=256)[:, j]
                        o = wt[:, to, :].rearrange("p (k j c b) -> p j c k b", k=KC, j=2, b=32)[:, j]
                    last = nc.vector.transpose(o, i)
                last.then_inc(wt_ready, 1)

            def compare_keys(g):
                dve.wait_ge(keys_psum, g + 1)
                if g:
                    dve.wait_ge(keys_compared, g)
                for j in range(EG):
                    c = EG * g + j
                    last = nc.vector.scalar_tensor_tensor(
                        out=junk[0:EP, j * EP:(j + 1) * EP], in0=misc[g % 2][0:EP, j * EP:(j + 1) * EP],
                        scalar=edge_work[:, 0, c:c + 1], in1=later[:, :], op0=ALU.is_equal, op1=ALU.mult,
                        accum_out=edge_work[:, 1, c:c + 1])
                last.then_inc(keys_compared, 1)

            def read_latest(g):
                dve.wait_ge(latest_psum, g + 1)
                nc.vector.tensor_reduce(latest_g[:, g, :], misc[2 + g % 2][0:N, 0:EG * N].rearrange(
                    "p (c n) -> p n c", c=EG), AX.X, ALU.max).then_inc(latest_read, 1)

            def build_mask():
                dve.wait_ge(latest_read, EC // EG)
                link(nc.vector.tensor_reduce(latest[:, :], latest_g[:, :, :].rearrange("p g n -> p n g"),
                                             AX.X, ALU.max))
                link(nc.vector.tensor_tensor(latest[:, :], latest[:, :], diag3[:, :], ALU.max))
                link(nc.vector.tensor_copy(latest_i[:, :], latest[:, :]))
                link(nc.vector.tensor_single_scalar(latest_i[:, :], latest_i[:, :], 3, op=ALU.bitwise_and))
                link(nc.vector.tensor_copy(mask_part[:, :], latest_i[:, :]))
                dve.wait_ge(etw_ln, 1)
                nc.vector.scalar_tensor_tensor(out=etw_soft[:, :], in0=etw_all[:, :], scalar=0.0,
                                               in1=etw_a[:, :], op0=ALU.max, op1=ALU.add)
                link(nc.vector.tensor_scalar(mask[:, :], latest[:, :], 2.5, NEG, ALU.is_lt, ALU.mult))
                for w in range(4):
                    link(nc.vector.tensor_scalar(gz[:, 0, :], mask_part[:, :], float(w),
                                                 etw_soft[:, w:w + 1], ALU.is_equal, ALU.mult))
                    ins = nc.vector.tensor_tensor(mask[:, :], mask[:, :], gz[:, 0, :], ALU.add)
                    if w < 3:
                        link(ins)
                    else:
                        ins.then_inc(mask_ready, 1)

            def mask_scores(b):
                dve.wait_ge(scores_psum, b + 1)
                for hh in HEADS_OF[b]:
                    s = slot_of(hh)
                    last = nc.vector.scalar_tensor_tensor(
                        out=probs[:, hh, :], in0=misc[b][0:N, s * N:(s + 1) * N], scalar=SCALE,
                        in1=mask[:, :], op0=ALU.mult, op1=ALU.add)
                link(last)
                heads = probs[:, HEADS_OF[b][0]:HEADS_OF[b][-1] + 1:2, :]
                nc.vector.tensor_reduce(col(NMAX + 4 * b, 4), heads, AX.X, ALU.max, negate=True
                                        ).then_inc(masked_ready, 1)

            def layernorm(turn, y, half_in):
                for half in range(2):
                    half_in(half)
                    ins = nc.vector.bn_stats(col(STAT + 6 * half, 6), y[:, half * HALF:(half + 1) * HALF])
                link(ins)
                link(nc.vector.bn_aggr(col(AGG, 2), small[0:N, STAT:STAT + 12]))
                nc.vector.tensor_scalar(col(VEPS), col(AGG + 1), EPS, None, ALU.add).then_inc(var_ready, 1)
                dve.wait_ge(rstd_guess, turn + 1)
                link(nc.vector.scalar_tensor_tensor(out=col(SQ), in0=col(GUESS), scalar=col(GUESS),
                                                    in1=col(VEPS), op0=ALU.mult, op1=ALU.mult))
                link(nc.vector.tensor_scalar(col(SQ), col(SQ), -0.5, 1.5, ALU.mult, ALU.add))
                link(nc.vector.tensor_tensor(col(RSTD), col(SQ), col(GUESS), ALU.mult))

            dve.wait_ge(x_in, 16)
            nc.vector.tensor_copy(x_band[:, :].rearrange("p (k a d) -> p a k d", k=KC, a=4),
                                  x_nodes[:, :].rearrange("p (a k d) -> p a k d", k=KC, a=4)
                                  ).then_inc(x_band_ready, 1)
            dve.wait_ge(etw_in, 16)
            nc.vector.scalar_tensor_tensor(out=etw_a[:, :], in0=etw_all[:, :], scalar=-1.0,
                                           in1=etw_all[:, :], op0=ALU.mult, op1=ALU.min).then_inc(etw_pre, 1)
            dve.wait_ge(edge_psum, 1)
            nc.vector.tensor_copy(edge_cols[:, :, :], misc[3][0:EP, 0:3 * EC].rearrange(
                "p (k c) -> p k c", k=3)).then_inc(edge_cols_ready, 1)
            dve.wait_ge(edge_cols_ready, 1)
            dve.wait_ge(pool_const, 1)
            nc.vector.scalar_tensor_tensor(out=edge_work[:, 0, :], in0=edge_cols[:, 0, :], scalar=float(N),
                                           in1=edge_cols[:, 1, :], op0=ALU.mult, op1=ALU.add)
            link(nc.vector.tensor_scalar(edge_work[:, 2, :], edge_cols[:, 2, :], 0.0, 4.0, ALU.is_equal,
                                         ALU.mult))
            link(nc.vector.tensor_tensor(edge_work[:, 2, :], edge_work[:, 2, :], edge_cols[:, 2, :], ALU.add))
            link(nc.vector.tensor_tensor(edge_work[:, 3, :], edge_work[:, 2, :], chunk_base[:, :], ALU.add))

            for tile in range(TILES):
                transpose_tile(tile)
                if 2 <= tile < 6:
                    compare_keys(2 * (tile - 2))
                    compare_keys(2 * (tile - 2) + 1)
                if tile == 5:
                    dve.wait_ge(keys_compared, EC // EG)
                    nc.vector.scalar_tensor_tensor(out=edge_work[:, 4, :], in0=edge_work[:, 1, :],
                                                   scalar=0.5, in1=edge_work[:, 3, :], op0=ALU.is_lt,
                                                   op1=ALU.mult).then_inc(kept_ready, 1)
                if 11 <= tile < 15:
                    read_latest(2 * (tile - 11))
                    read_latest(2 * (tile - 11) + 1)
                if tile == 15:
                    dve.wait_ge(count_psum, 1)
                    nc.vector.tensor_copy(countT[:, :], wide[0][0:N, 0:N]).then_inc(count_ready, 1)
                    dve.wait_ge(count_ready, 1)
                    nc.vector.tensor_scalar(absentT[:, :], countT[:, :], 0.5, NEG, ALU.is_lt, ALU.mult)
                    build_mask()
                    dve.wait_ge(mask_ready, 1)
                if 16 <= tile < 20:
                    mask_scores(tile - 16)
            dve.wait_ge(probs_ready, HEADS)
            link(nc.vector.reciprocal(col(ROWINV, HEADS), col(ROWSUM, HEADS)))
            for half in range(2):
                dve.wait_ge(mix_psum, half + 1)
                for a in (2 * half, 2 * half + 1):
                    band = mixed[:, :].rearrange("p (h e a d) -> p a h e d", h=4, e=2, a=4)[:, a]
                    heads = acc[half][0:N, (a % 2) * TR:(a % 2 + 1) * TR]
                    nc.vector.tensor_tensor(
                        band, heads.rearrange("p (h e d) -> p h e d", h=4, e=2),
                        col(ROWINV + 4 * a, 4).rearrange("p (h e d) -> p h e d", e=1, d=1)
                        .to_broadcast([N, 4, 2, 32]), ALU.mult).then_inc(mixed_ready, 1)
            for g in range(2):
                dve.wait_ge(oT_psum, g + 1)
                nc.vector.tensor_tensor(
                    oT[:, 4 * g:4 * g + 4, :], misc[g][:, 0:4 * N].rearrange("p (c n) -> p c n", c=4),
                    biasT[:, 3 * KC + 4 * g:3 * KC + 4 * g + 4].rearrange("p (c n) -> p c n", n=1)
                    .to_broadcast([P, 4, N]), ALU.add).then_inc(oT_ready, 1)

            def residual_1(half):
                dve.wait_ge(tile_done, T_WO + 2 * half + 2)
                if half == 0:
                    dve.wait_ge(x_bo_ready, 1)
                span = slice(half * HALF, (half + 1) * HALF)
                link(nc.vector.tensor_tensor(y1[:, span], wide[half][0:N, :], x_bo[:, span], ALU.add))

            layernorm(0, y1, residual_1)
            for half in range(2):
                span = slice(half * HALF, (half + 1) * HALF)
                nc.vector.tensor_scalar(x1[:, span], y1[:, span], col(AGG), col(RSTD), ALU.subtract,
                                        ALU.mult).then_inc(x1_ready, 1)
            dve.wait_ge(x1T_psum, 1)
            nc.vector.tensor_copy(x1T[:, 0:4, :], misc[2][:, 0:4 * N].rearrange("p (c n) -> p c n", c=4)
                                  ).then_inc(x1T_ready, 1)
            dve.wait_ge(gat_a_in, 16)
            for half in range(2):
                dve.wait_ge(h_ready, half + 1)
                span = slice(half * HALF, (half + 1) * HALF)
                for side in range(2):
                    ins = nc.vector.scalar_tensor_tensor(
                        out=junk[0:N, :], in0=h[:, span], scalar=1.0, in1=gat_a_all[:, side, span],
                        op0=ALU.mult, op1=ALU.mult, accum_out=col(DOTS + 2 * half + side))
                    link(ins)
            nc.vector.tensor_tensor(col(AL, 2), col(DOTS, 2), col(DOTS + 2, 2), ALU.add
                                    ).then_inc(logits_ready, 1)
            dve.wait_ge(spread_psum, 1)
            link(nc.vector.tensor_scalar(gz[:, 0, :], misc[0][0:N, 0:N], col(AL + 1), None, ALU.add))
            link(nc.vector.scalar_tensor_tensor(out=gz[:, 3, :], in0=gz[:, 0, :], scalar=0.1,
                                                in1=gz[:, 0, :], op0=ALU.mult, op1=ALU.max))
            nc.vector.scalar_tensor_tensor(out=gz[:, 1, :], in0=gz[:, 3, :], scalar=-1.0, in1=absentT[:, :],
                                           op0=ALU.mult, op1=ALU.add).then_inc(gexp_in, 1)
            dve.wait_ge(gexp_out, 1)
            nc.vector.tensor_tensor(gz[:, 3, :], gz[:, 2, :], countT[:, :], ALU.mult).then_inc(adj_ready, 1)
            dve.wait_ge(degree_psum, 1)
            link(nc.vector.tensor_scalar(col(INV + 1), misc[1][0:N, 0:1], EPS, None, ALU.add))
            nc.vector.reciprocal(col(INV), col(INV + 1)).then_inc(inv_ready, 1)

            def residual_2(half):
                span = slice(half * HALF, (half + 1) * HALF)
                dve.wait_ge(elu_done, 2 * half + 2)
                if half == 0:
                    dve.wait_ge(x1m1_ready, 1)
                link(nc.vector.scalar_tensor_tensor(out=y2[:, span], in0=elu_e[:, span], scalar=1.0,
                                                    in1=x1m1[:, span], op0=ALU.min, op1=ALU.add))
                link(nc.vector.tensor_tensor(y2[:, span], y2[:, span], elu_r[:, span], ALU.add))

            layernorm(1, y2, residual_2)
            for half in range(2):
                span = slice(half * HALF, (half + 1) * HALF)
                nc.vector.tensor_scalar(final[:, span], y2[:, span], col(AGG), col(RSTD), ALU.subtract,
                                        ALU.mult).then_inc(final_ready, 1)

        @block.tensor
        def _(pe):
            pe.wait_ge(ident_ready, 1)
            pe.wait_ge(x_band_ready, 1)
            for k in range(KC):
                last = nc.tensor.transpose(misc[k // 4][:, (k % 4) * N:(k % 4 + 1) * N], x_band[:, k * P:(k + 1) * P],
                                           ident[0:N, 0:N])
                if k % 4 == 3:
                    last.then_inc(xT_psum, 1)
            pe.wait_ge(bias_in, 16 * NB)
            nc.tensor.transpose(misc[2][:, 0:NB * KC], bias_rows[:, :], ident[0:NB * KC, 0:NB * KC]
                                ).then_inc(bias_psum, 1)
            pe.wait_ge(edge_conv, 1)
            for k in range(3):
                last = nc.tensor.transpose(misc[3][0:EP, k * EC:(k + 1) * EC], edge_rows[:, k, :],
                                           ident[0:EC, 0:EC])
            last.then_inc(edge_psum, 1)

            def column_products(tile, rhs):
                turn = tile
                m, slot = matrix_of(tile), tile % NWT
                pe.wait_ge(wt_ready, tile + 1)
                if turn >= 2:
                    pe.wait_ge(acc_read, turn - 1)
                for j in range(2):
                    for k in range(KC):
                        last = nc.tensor.matmul(acc[turn % 2][:, j * N:(j + 1) * N],
                                                wt[:, slot, k * TR + j * P:k * TR + (j + 1) * P],
                                                rhs[:, k, :], start=(k == 0), stop=(k == KC - 1))
                last.then_inc(tile_done, 1)

            def row_products(tile, lhsT):
                slot, t = tile % NWT, tile % TPM
                pe.wait_ge(wt_ready, tile + 1)
                for k in range(KC):
                    last = nc.tensor.matmul(wide[t // 2][0:N, (t % 2) * TR:(t % 2 + 1) * TR],
                                            lhsT[:, k, :], wt[:, slot, k * TR:(k + 1) * TR],
                                            start=(k == 0), stop=(k == KC - 1))
                last.then_inc(tile_done, 1)

            def spread_keys(g):
                if g >= 2:
                    pe.wait_ge(keys_compared, g - 1)
                span = slice(g * EG * EP, (g + 1) * EG * EP)
                nc.tensor.matmul(misc[g % 2][0:EP, 0:EG * EP], times_n[:, :], key_src[:, span],
                                 start=True, stop=False)
                nc.tensor.matmul(misc[g % 2][0:EP, 0:EG * EP], times_1[:, :], key_dst[:, span],
                                 start=False, stop=True).then_inc(keys_psum, 1)

            def latest_edges(g):
                if g >= 2:
                    pe.wait_ge(latest_read, g - 1)
                for j in range(EG):
                    last = nc.tensor.matmul(misc[2 + g % 2][0:N, j * N:(j + 1) * N], src_hot[:, EG * g + j, :],
                                            dst_val[:, EG * g + j, :], start=True, stop=True)
                last.then_inc(latest_psum, 1)

            sources = {T_WQ: xT, T_WK: xT, T_WIQ: qT, T_WIK: kT, T_WV: xT}
            pe.wait_ge(xT_ready, 2)
            for tile in range(T_WIV):
                if tile == T_WIQ:
                    pe.wait_ge(acc_read, T_WK)
                if tile == T_WIK:
                    pe.wait_ge(acc_read, T_WIQ)
                column_products(tile, sources[matrix_of(tile)])
                if tile == 1:
                    pe.wait_ge(keys_placed, 2)
                    pe.wait_ge(pool_const, 1)
                    pe.wait_ge(bias_ready, 1)
                if 1 <= tile < 5:
                    spread_keys(2 * (tile - 1))
                    spread_keys(2 * (tile - 1) + 1)
                if tile == 10:
                    pe.wait_ge(val_ready, 1)
                    pe.wait_ge(hot_ready, 2)
                if 10 <= tile < 14:
                    latest_edges(2 * (tile - 10))
                    latest_edges(2 * (tile - 10) + 1)
                if tile == T_WV - 2:
                    for c in range(EC):
                        last = nc.tensor.matmul(wide[0][0:N, 0:N], dst_hot[:, c, :], src_hot[:, c, :],
                                                start=(c == 0), stop=(c == EC - 1))
                    last.then_inc(count_psum, 1)
                if tile == T_WV - 1:
                    pe.wait_ge(acc_read, T_WV)
                    pe.wait_ge(keys_compared, EC // EG)
                    pe.wait_ge(latest_read, EC // EG)
                    for b in range(4):
                        for hh in HEADS_OF[b]:
                            rows = slice(HD * (hh % 2), HD * (hh % 2) + HD)
                            last = nc.tensor.matmul(misc[b][0:N, slot_of(hh) * N:(slot_of(hh) + 1) * N],
                                                    q2T[rows, hh // 2, :], k2T[rows, hh // 2, :],
                                                    start=True, stop=True)
                        last.then_inc(scores_psum, 1)
            pe.wait_ge(masked_ready, 4)
            for b in range(4):
                for hh in HEADS_OF[b]:
                    pe.wait_ge(probs_ready, HEAD_ORDER.index(hh) + 1)
                    last = nc.tensor.transpose(misc[b][0:N, slot_of(hh) * N:(slot_of(hh) + 1) * N],
                                               probs[:, hh, :], ident[0:N, 0:N])
                last.then_inc(probsT_psum, 1)
            pe.wait_ge(acc_read, T_WIV)
            pe.wait_ge(count_ready, 1)
            for tile in range(T_WIV, T_WO):
                row_products(tile, vT)
            pe.wait_ge(probsT_ready, 4)
            for half in range(2):
                pe.wait_ge(wide_read, half + 1)
                for hh in range(8 * half, 8 * half + 8):
                    last = nc.tensor.matmul(acc[half][0:N, (hh % 8) * HD:(hh % 8 + 1) * HD],
                                            probsT[:, 4 * bank_of(hh) + slot_of(hh), :],
                                            v2[:, hh * HD:(hh + 1) * HD], start=True, stop=True)
                last.then_inc(mix_psum, 1)
            pe.wait_ge(mixed_ready, 4)
            for k in range(KC):
                last = nc.tensor.transpose(misc[k // 4][:, (k % 4) * N:(k % 4 + 1) * N], mixed[:, k * P:(k + 1) * P],
                                           ident[0:N, 0:N])
                if k % 4 == 3:
                    last.then_inc(oT_psum, 1)
            pe.wait_ge(oT_ready, 2)
            for tile in range(T_WO, TILES):
                row_products(tile, oT)
            for k in range(KC):
                if k % 4 == 0:
                    pe.wait_ge(x1_ready, k // 4 + 1)
                last = nc.tensor.transpose(misc[2 + k // 4][:, (k % 4) * N:(k % 4 + 1) * N],
                                           x1[:, k * P:(k + 1) * P], ident[0:N, 0:N])
                if k % 4 == 3:
                    last.then_inc(x1T_psum, 1)
            pe.wait_ge(x1T_ready, 2)
            pe.wait_ge(gat_w_in, 64)
            for half in range(2):
                for k in range(KC):
                    last = nc.tensor.matmul(acc[half][0:N, :], x1T[:, k, :],
                                            gat_w_sb[:, k, half * HALF:(half + 1) * HALF],
                                            start=(k == 0), stop=(k == KC - 1))
                last.then_inc(h_psum, 1)
            pe.wait_ge(logits_ready, 1)
            nc.tensor.matmul(misc[0][0:N, 0:N], col(AL).to_broadcast([N, N]), ident[0:N, 0:N],
                             start=True, stop=True).then_inc(spread_psum, 1)
            pe.wait_ge(adj_ready, 1)
            nc.tensor.matmul(misc[1][0:N, 0:1], gz[:, 3, :], col(ONE), start=True, stop=True
                             ).then_inc(degree_psum, 1)
            for half in range(2):
                nc.tensor.matmul(wide[half][0:N, :], gz[:, 3, :], h[:, half * HALF:(half + 1) * HALF],
                                 start=True, stop=True).then_inc(agg_psum, 1)


_INS = ['x', 'src', 'dst', 'edge_type_5', 'L0_gnn_edge_type_weights', 'L0_gnn_wq', 'L0_gnn_bq', 'L0_gnn_wk',
        'L0_gnn_bk', 'L0_gnn_wv', 'L0_gnn_bv', 'L0_gnn_wiq', 'L0_gnn_biq', 'L0_gnn_wik', 'L0_gnn_bik',
        'L0_gnn_wiv', 'L0_gnn_biv', 'L0_gnn_wo', 'L0_gnn_bo', 'L1_gnn_W', 'L1_gnn_a']


def kernel(**inputs):
    import numpy as _np
    import concourse.bacc as _bacc
    from concourse import mybir as _mybir
    from concourse.bass_utils import run_bass_kernel_spmd as _run

    nc = _bacc.Bacc("TRN2", target_bir_lowering=False, num_devices=1)
    arrays, args = {}, []
    for name in _INS:
        a = _np.ascontiguousarray(inputs[name])
        arrays[f"in_{name}"] = a
        args.append(nc.dram_tensor(f"in_{name}", a.shape, _mybir.dt.from_np(a.dtype), kind="ExternalInput").ap())
    out = nc.dram_tensor("out_0", (96, 1024), _mybir.dt.float32, kind="ExternalOutput").ap()
    build(nc, *args, out)
    r = _run(nc, [arrays], core_ids=[0])
    return r.results[0]["out_0"]
```

```python
import concourse.bass as bass
from concourse import mybir
from contextlib import ExitStack


def build(nc, x, src, dst, edge_type_5, etw, wq, bq, wk, bk, wv, bv, wiq, biq, wik, bik, wiv, biv, wo, bo,
          gat_w, gat_a, out):
    f32, bf16, i32 = mybir.dt.float32, mybir.dt.bfloat16, mybir.dt.int32
    ALU, ACT, AX = mybir.AluOpType, mybir.ActivationFunctionType, mybir.AxisListType

    N, F = x.shape
    P = 128
    KC = F // P
    HEADS, HD = 16, F // 16
    HALF = F // 2
    SCALE = HD ** -0.5
    EC = 32
    EP = src.shape[0] // EC
    EG = 4
    WARM_UP = 16
    NEG = -1.0e30
    EPS = 1e-5

    TR = 256
    TPM = F // TR
    NRAW, NWT = 6, 6
    STREAM = [wq, wk, wiq, wik, wv, wiv, wo]
    TILES = TPM * len(STREAM)
    T_WQ, T_WK, T_WIQ, T_WIK, T_WV, T_WIV, T_WO = [TPM * m for m in range(7)]
    BANDED_OUT = (T_WQ, T_WK, T_WV, T_WO)

    GAT_W_AFTER = (T_WIV + 1, T_WIV + 3, T_WO + 1, T_WO + 3)

    DOTS_AFTER = (T_WIV + 2, T_WO)

    def matrix_of(tile):
        return tile - tile % TPM

    ctx = ExitStack()
    with ctx:
        def sb(name, shape, dt=f32):
            return ctx.enter_context(nc.sbuf_tensor(name, shape, dt))

        def ps(name):
            return ctx.enter_context(nc.psum_tensor(name, [P, 512], f32))

        def sem(name):
            return ctx.enter_context(nc.semaphore(name))

        raw = sb("raw", [P, NRAW, KC * TR])
        wt = sb("wt", [P, NWT, KC * TR])
        gat_w_sb = sb("gat_w_sb", [P, KC, F])
        x_nodes = sb("x_nodes", [N, F])
        scratch = sb("scratch", [P, F])
        xT = sb("xT", [P, KC, N])
        qT = sb("qT", [P, KC, N])
        kT = sb("kT", [P, KC, N])
        vT = sb("vT", [P, KC, N])
        q2T = sb("q2T", [P, KC, N])
        k2T = sb("k2T", [P, KC, N])
        v2 = sb("v2", [N, F])
        probs = sb("probs", [N, HEADS, N])
        probsT = sb("probsT", [N, HEADS, N])
        mixed = sb("mixed", [N, F])
        gat_a_all = sb("gat_a_all", [P, 2, F])
        wsum = sb("wsum", [P, F])
        wa = sb("wa", [P, 2, KC])
        wa_sum = sb("wa_sum", [P, 2])
        wa_prod = sb("wa_prod", [P, F])
        ones = sb("ones", [P, N])
        mean_rows = sb("mean_rows", [P, N])
        logit_parts = sb("logit_parts", [N, 4])
        ident = sb("ident", [P, P])
        NB = 7
        bias_rows = sb("bias_rows", [NB * KC, P])
        biasT = sb("biasT", [P, NB * KC])
        small = sb("small", [P, 256])
        edge_rows_i = sb("edge_rows_i", [EC, 3, EP], i32)
        edge_rows = sb("edge_rows", [EC, 3, EP])
        edge_rows_b = sb("edge_rows_b", [EC, 2, EP], bf16)
        edge_cols = sb("edge_cols", [EP, 3, EC])
        edge_work = sb("edge_work", [EP, 5, EC])
        times_n = sb("times_n", [EC, EP], bf16)
        times_1 = sb("times_1", [EC, EP], bf16)
        later = sb("later", [EP, EP])
        node_ids = sb("node_ids", [EP, N])
        chunk_base = sb("chunk_base", [EP, EC])
        diag3 = sb("diag3", [N, N])
        latest_g = sb("latest_g", [N, EC // EG, N])
        latest = sb("latest", [N, N])
        latest_i = sb("latest_i", [N, N], i32)
        mask = sb("mask", [N, N])
        mask_part = sb("mask_part", [N, N])
        countT = sb("countT", [N, N])
        absentT = sb("absentT", [N, N])
        etw_all = sb("etw_all", [N, 4])
        etw_a = sb("etw_a", [N, 4])
        etw_soft = sb("etw_soft", [N, 4])
        gz = sb("gz", [N, 5, N])
        region = gat_w_sb[:, :, :].rearrange("p k n -> p (k n)").bitcast(bf16)
        key_src = region[0:EC, 0:EC * EP]
        key_dst = region[0:EC, EC * EP:2 * EC * EP]
        at = 2 * EC * EP
        src_hot = region[0:EP, at:at + EC * N].rearrange("p (c n) -> p c n", c=EC)
        dst_hot = region[0:EP, at + EC * N:at + 2 * EC * N].rearrange("p (c n) -> p c n", c=EC)
        dst_val = region[0:EP, at + 2 * EC * N:at + 3 * EC * N].rearrange("p (c n) -> p c n", c=EC)

        x_band = scratch[0:N, :]
        junk = scratch
        oT = qT
        yT = vT
        x1 = x_nodes
        h = v2
        elu_e = mixed
        elu_r = gat_a_all[0:N, 0, :]
        y2 = probs[:, :, :].rearrange("p h n -> p (h n)")[:, 0:F]
        final = probsT[:, :, :].rearrange("p h n -> p (h n)")[:, 0:F]

        acc = [ps(f"acc{i}") for i in range(2)]
        wide = [ps(f"wide{i}") for i in range(2)]
        misc = [ps(f"misc{i}") for i in range(4)]

        raw_in = [sem(f"raw_in{i}") for i in range(NRAW)]
        x_in, bias_in, edge_in, etw_in = sem("x_in"), sem("bias_in"), sem("edge_in"), sem("etw_in")
        first_in = [sem(f"first_in{j}") for j in range(2)]
        gat_w_in = [sem(f"gat_w_in{g}") for g in range(4)]
        gat_a_in, out_done = sem("gat_a_in"), sem("out_done")
        wt_ready, tile_done = sem("wt_ready"), sem("tile_done")
        acc_read, wide_read = sem("acc_read"), sem("wide_read")
        x_band_ready = sem("x_band_ready")
        ident_ready, xT_psum, xT_ready, bias_psum, bias_ready = (
            sem("ident_ready"), sem("xT_psum"), sem("xT_ready"), sem("bias_psum"), sem("bias_ready"))
        pool_const, edge_conv, edge_psum, edge_cols_ready, keys_placed = (
            sem("pool_const"), sem("edge_conv"), sem("edge_psum"), sem("edge_cols_ready"), sem("keys_placed"))
        keys_psum, keys_compared, kept_ready, hot_ready, val_ready = (
            sem("keys_psum"), sem("keys_compared"), sem("kept_ready"), sem("hot_ready"), sem("val_ready"))
        latest_psum, latest_read, count_psum, count_ready = (
            sem("latest_psum"), sem("latest_read"), sem("count_psum"), sem("count_ready"))
        etw_pre, etw_ln, mask_ready = sem("etw_pre"), sem("etw_ln"), sem("mask_ready")
        scores_psum, masked_ready, probs_ready, probsT_psum, probsT_ready = (
            sem("scores_psum"), sem("masked_ready"), sem("probs_ready"), sem("probsT_psum"),
            sem("probsT_ready"))
        mix_psum, mixed_ready, oT_psum, oT_ready = (
            sem("mix_psum"), sem("mixed_ready"), sem("oT_psum"), sem("oT_ready"))
        yT_ready, y_psum, var_ready, x1_ready = (
            sem("yT_ready"), sem("y_psum"), sem("var_ready"), sem("x1_ready"))
        wsum_ready, wa_ready, wa_sum_ready, neg_mean_ready, mean_psum, mean_rows_ready, rstd_ready = (
            sem("wsum_ready"), sem("wa_ready"), sem("wa_sum_ready"), sem("neg_mean_ready"),
            sem("mean_psum"), sem("mean_rows_ready"), sem("rstd_ready"))
        h_psum, h_ready, dots_psum, logits_ready, spread_psum, gexp_in, gexp_out, adj_ready = (
            sem("h_psum"), sem("h_ready"), sem("dots_psum"), sem("logits_ready"), sem("spread_psum"),
            sem("gexp_in"), sem("gexp_out"), sem("adj_ready"))
        wa_prod_ready, wa1_ready, pow_ready = sem("wa_prod_ready"), sem("wa1_ready"), sem("pow_ready")
        agg_psum, degree_psum = sem("agg_psum"), sem("degree_psum")
        inv_ready, elu_done, final_ready = sem("inv_ready"), sem("elu_done"), sem("final_ready")
        pool_chain, dve_chain, act_chain = sem("pool_chain"), sem("dve_chain"), sem("act_chain")

        STAT, AGG, VEPS, RSTD, NEGM, MHALF = 0, 12, 14, 18, 19, 20
        ROWSUM, ROWINV, NMAX, DOTS, AL, INV = 32, 48, 64, 80, 84, 86

        def col(c, w=1, p=N):
            return small[0:p, c:c + w]

        def bank_of(head):
            return (head % 2) * 2 + head // 8

        def slot_of(head):
            return (head // 2) % 4

        HEADS_OF = [[hh for hh in range(HEADS) if bank_of(hh) == b] for b in range(4)]
        HEAD_ORDER = [hh for b in range(4) for hh in HEADS_OF[b]]

        def quarter(t, n):
            return t[0:N, 0:4 * n].rearrange("p (c n) -> p c n", c=4)

        block = ctx.enter_context(nc.Block())

        @block.sync
        def _(sp):
            def load_tile(tile):
                m, t, slot = matrix_of(tile), tile % TPM, tile % NRAW
                w = STREAM[tile // TPM]
                if m in BANDED_OUT:
                    rows = w.rearrange("(c t b) i -> t b c i", c=8, t=TPM, b=32)[t]
                else:
                    rows = w.rearrange("(t c b) i -> t b c i", c=8, t=TPM, b=32)[t]
                if tile >= NRAW:
                    sp.wait_ge(wt_ready, 2 * (tile - NRAW + 1))
                for a in range(4):
                    to = raw[32 * a:32 * a + 32, slot, :].rearrange("p (c i) -> p c i", c=8)
                    if m == T_WO:
                        for g in range(2):
                            i0 = 512 * g + 128 * a
                            sp.dma_start(to[:, :, 128 * g:128 * g + 128], rows[:, :, i0:i0 + 128]
                                         ).then_inc(raw_in[slot], 16)
                    else:
                        sp.dma_start(to, rows[:, :, 256 * a:256 * a + 256]).then_inc(raw_in[slot], 16)

            def load_first_tile():
                rows = wq.rearrange("(A j t b) i -> t j b A i", A=4, j=2, t=TPM, b=32)[0]
                for j in range(2):
                    for a in range(4):
                        to = raw[32 * a:32 * a + 32, 0, :].rearrange("p (A j i) -> p j A i", A=4, j=2)
                        sp.dma_start(to[:, j], rows[j, :, :, 256 * a:256 * a + 256]
                                     ).then_inc(first_in[j], 16)

            def load_gat_w(g):
                if g == 0:
                    sp.wait_ge(count_psum, 1)
                    sp.wait_ge(latest_psum, EC // EG)
                gw = gat_w.rearrange("(a k b) n -> a b k n", a=4, k=KC)
                for a in range(4):
                    sp.dma_start(gat_w_sb[32 * a:32 * a + 32, 2 * g:2 * g + 2, :],
                                 gw[a, :, 2 * g:2 * g + 2, :]).then_inc(gat_w_in[g], 16)

            sp.dma_start(x_nodes[:, :], x).then_inc(x_in, 16)
            load_first_tile()
            for tile in range(1, TILES):
                load_tile(tile)
                if tile in GAT_W_AFTER:
                    load_gat_w(GAT_W_AFTER.index(tile))
            for half in range(2):
                sp.wait_ge(final_ready, half + 1)
                sp.dma_start(out[:, half * HALF:(half + 1) * HALF],
                             final[:, half * HALF:(half + 1) * HALF]).then_inc(out_done, 16)
            sp.wait_ge(out_done, 32)

        @block.gpsimd
        def _(pool):
            links = [0]

            def link(ins):
                links[0] += 1
                ins.then_inc(pool_chain, 1)
                pool.wait_ge(pool_chain, links[0])

            link(nc.gpsimd.memset(ident[:, :], 0.0))
            nc.gpsimd.affine_select(out=ident[:, :], in_=ident[:, :], compare_op=ALU.not_equal, fill=1.0,
                                    base=0, pattern=[[-1, P]], channel_multiplier=1).then_inc(ident_ready, 1)
            for m, b in enumerate((bq, bk, bv, bo)):
                pool.dma_start(bias_rows[KC * m:KC * m + KC, :].rearrange("k (a d) -> k a d", a=4),
                               b.rearrange("(a k d) -> k a d", a=4, k=KC)).then_inc(bias_in, 16)
            for m, b in enumerate((biq, bik)):
                pool.dma_start(bias_rows[KC * (4 + m):KC * (5 + m), :],
                               b.rearrange("(k p) -> k p", p=P)).then_inc(bias_in, 16)
            for g in range(2):
                pool.dma_start(bias_rows[KC * 6 + 4 * g:KC * 6 + 4 * g + 4, :]
                               .rearrange("k (a d) -> k a d", a=4),
                               biv.rearrange("(g a k d) -> g k a d", g=2, a=4, k=4)[g]
                               ).then_inc(bias_in, 16)
            pool.dma_start(etw_all[:, :], etw.rearrange("(o n) -> o n", o=1).to_broadcast([N, 4])
                           ).then_inc(etw_in, 16)
            link(nc.gpsimd.memset(later[:, :], 1.0))
            link(nc.gpsimd.memset(diag3[:, :], 0.0))
            nc.gpsimd.memset(ones[:, :], 1.0)
            nc.gpsimd.memset(small[:, MHALF:MHALF + 1], -0.5)
            nc.gpsimd.memset(times_n[:, :], float(N))
            nc.gpsimd.memset(times_1[:, :], 1.0)
            nc.gpsimd.iota(node_ids[:, :], pattern=[[1, N]], base=0, channel_multiplier=0,
                           allow_small_or_imprecise_dtypes=True)
            nc.gpsimd.iota(chunk_base[:, :], pattern=[[4, EC]], base=3, channel_multiplier=0,
                           allow_small_or_imprecise_dtypes=True)
            nc.gpsimd.affine_select(out=later[:, :], in_=later[:, :], compare_op=ALU.is_gt, fill=0.0,
                                    base=0, pattern=[[1, EP]], channel_multiplier=-1)
            nc.gpsimd.affine_select(out=diag3[:, :], in_=diag3[:, :], compare_op=ALU.not_equal, fill=3.0,
                                    base=0, pattern=[[-1, N]], channel_multiplier=1).then_inc(pool_const, 1)
            pool.wait_ge(edge_in, 48)
            nc.gpsimd.tensor_copy(edge_rows[:, :, :], edge_rows_i[:, :, :]).then_inc(edge_conv, 1)
            link(nc.gpsimd.tensor_copy(edge_rows_b[:, :, :], edge_rows_i[:, 0:2, :]))
            for k, place in enumerate((key_src, key_dst)):
                nc.gpsimd.affine_select(out=place.rearrange("p (c e) -> p c e", c=EC),
                                        in_=edge_rows_b[:, k:k + 1, :].to_broadcast([EC, EC, EP]),
                                        compare_op=ALU.is_equal, fill=0.0, base=0,
                                        pattern=[[1, EC], [0, EP]], channel_multiplier=-1
                                        ).then_inc(keys_placed, 1)
            pool.wait_ge(edge_cols_ready, 1)
            pool.wait_ge(pool_const, 1)
            for k, hot in enumerate((src_hot, dst_hot)):
                link(nc.gpsimd.tensor_tensor(hot, node_ids[:, :].rearrange("p (c n) -> p c n", c=1)
                                        .to_broadcast([EP, EC, N]),
                                        edge_cols[:, k, :].rearrange("p (c n) -> p c n", n=1)
                                        .to_broadcast([EP, EC, N]), ALU.subtract))
                nc.gpsimd.tensor_scalar(hot, hot, 0.0, None, ALU.is_equal).then_inc(hot_ready, 1)
            pool.wait_ge(hot_ready, 2)
            pool.wait_ge(kept_ready, 1)
            nc.gpsimd.tensor_tensor(dst_val, dst_hot,
                                    edge_work[:, 4, :].rearrange("p (c n) -> p c n", n=1)
                                    .to_broadcast([EP, EC, N]), ALU.mult).then_inc(val_ready, 1)
            pool.dma_start(gat_a_all[:, :, :].rearrange("p a n -> p (a n)"), gat_a.to_broadcast([P, 2 * F])
                           ).then_inc(gat_a_in, 16)
            pool.wait_ge(gat_a_in, 16)
            for g in range(4):
                pool.wait_ge(gat_w_in[g], 64)
                for k in (2 * g, 2 * g + 1):
                    if k:
                        pool.wait_ge(wa1_ready, k)
                    nc.gpsimd.tensor_tensor(wa_prod[:, :], gat_w_sb[:, k, :], gat_a_all[:, 1, :], ALU.mult
                                            ).then_inc(wa_prod_ready, 1)
                    if k == 0:
                        continue
                    first = gat_w_sb[:, 0, :] if k == 1 else wsum[:, :]
                    ins = nc.gpsimd.tensor_tensor(wsum[:, :], first, gat_w_sb[:, k, :], ALU.add)
                    if k < KC - 1:
                        link(ins)
                    else:
                        ins.then_inc(wsum_ready, 1)
            for turn in range(2):
                pool.wait_ge(var_ready, turn + 1)
                nc.gpsimd.tensor_tensor(col(RSTD), col(VEPS), col(MHALF), ALU.pow).then_inc(rstd_ready, 1)

        @block.scalar
        def _(act):
            links = [0]

            def link(ins):
                links[0] += 1
                ins.then_inc(act_chain, 1)
                act.wait_ge(act_chain, links[0])

            nc.scalar.preload_act_table_set("natural_log_exp_and_others")
            for g in range(2):
                act.wait_ge(xT_psum, g + 1)
                nc.scalar.activation(xT[:, 4 * g:4 * g + 4, :], misc[g][:, 0:4 * N].rearrange(
                    "p (c n) -> p c n", c=4), ACT.Copy).then_inc(xT_ready, 1)
            for k, e in enumerate((src, dst, edge_type_5)):
                act.dma_start(edge_rows_i[:, k, :], e.rearrange("(c e) -> c e", c=EC)).then_inc(edge_in, 16)
            act.wait_ge(bias_psum, 1)
            nc.scalar.activation(biasT[:, :], misc[2][:, 0:NB * KC], ACT.Copy).then_inc(bias_ready, 1)
            act.wait_ge(etw_pre, 1)
            link(nc.scalar.activation(etw_a[:, :], etw_a[:, :], ACT.Exp))
            nc.scalar.activation(etw_a[:, :], etw_a[:, :], ACT.Ln, bias=1.0).then_inc(etw_ln, 1)
            act.wait_ge(bias_ready, 1)

            dest = {T_WQ: (qT, 0), T_WK: (kT, 1), T_WIQ: (q2T, 4), T_WIK: (k2T, 5), T_WV: (vT, 2)}

            def evacuate(tile, turn):
                act.wait_ge(tile_done, tile + 1)
                m, t = matrix_of(tile), tile % TPM
                to, brow = dest[m]
                for j in range(2):
                    chunk = 4 * j + t if m in BANDED_OUT else 2 * t + j
                    last = nc.scalar.activation(to[:, chunk, :], acc[turn % 2][:, j * N:(j + 1) * N],
                                                ACT.Identity,
                                                bias=biasT[:, KC * brow + chunk:KC * brow + chunk + 1])
                last.then_inc(acc_read, 1)

            def exps(b):
                act.wait_ge(masked_ready, b + 1)
                for hh in HEADS_OF[b]:
                    nc.scalar.activation(probs[:, hh, :], probs[:, hh, :], ACT.Exp,
                                         bias=col(NMAX + 4 * b + slot_of(hh)),
                                         accum_out=col(ROWSUM + hh)).then_inc(probs_ready, 1)

            for tile in range(T_WIV):
                evacuate(tile, tile)
                if tile > T_WV:
                    exps(tile - T_WV - 1)
            exps(3)
            for b in range(4):
                act.wait_ge(probsT_psum, b + 1)
                nc.scalar.activation(probsT[:, 4 * b:4 * b + 4, :], quarter(misc[b], N), ACT.Copy
                                     ).then_inc(probsT_ready, 1)
            def add_up(k):
                act.wait_ge(wa_prod_ready, k + 1)
                nc.scalar.activation(wa_prod[:, :], wa_prod[:, :], ACT.Copy, accum_out=wa[:, 1, k:k + 1]
                                     ).then_inc(wa1_ready, 1)

            add_up(0)
            add_up(1)
            for half in range(2):
                act.wait_ge(tile_done, T_WIV + 2 * half + 2)
                nc.scalar.activation(v2[:, half * HALF:(half + 1) * HALF], wide[half][0:N, :], ACT.Copy
                                     ).then_inc(wide_read, 1)
                add_up(2 + half)
            for k in range(4, KC):
                add_up(k)
            act.wait_ge(mean_psum, 1)
            nc.scalar.activation(mean_rows[:, :], misc[1][:, 0:N], ACT.Copy).then_inc(mean_rows_ready, 1)
            act.wait_ge(rstd_ready, 1)

            def evacuate_h(half):
                act.wait_ge(h_psum, half + 1)
                nc.scalar.activation(h[:, half * HALF:(half + 1) * HALF], acc[half][0:N, :], ACT.Copy,
                                     scale=col(RSTD)).then_inc(h_ready, 1)

            def elu_parts(half):
                act.wait_ge(agg_psum, half + 1)
                span = slice(half * HALF, (half + 1) * HALF)
                nc.scalar.activation(elu_e[:, span], wide[half][0:N, :], ACT.Exp, scale=col(INV)
                                     ).then_inc(elu_done, 1)
                nc.scalar.activation(elu_r[:, span], wide[half][0:N, :], ACT.Relu, scale=col(INV)
                                     ).then_inc(elu_done, 1)

            act.wait_ge(gexp_in, 1)
            nc.scalar.activation(gz[:, 2, :], gz[:, 1, :], ACT.Exp).then_inc(gexp_out, 1)
            evacuate_h(0)
            act.wait_ge(inv_ready, 1)
            elu_parts(0)
            evacuate_h(1)
            elu_parts(1)

        @block.vector
        def _(dve):
            links = [0]

            def link(ins):
                links[0] += 1
                ins.then_inc(dve_chain, 1)
                dve.wait_ge(dve_chain, links[0])

            arrived = [0] * NRAW

            def transpose_tile(tile):
                m, slot, to = matrix_of(tile), tile % NRAW, tile % NWT
                arrived[slot] += 0 if tile == 0 else 128 if m == T_WO else 64
                if arrived[slot]:
                    dve.wait_ge(raw_in[slot], arrived[slot])
                if tile >= NWT:
                    dve.wait_ge(tile_done, tile - NWT + 1)
                for j in range(2):
                    if tile == 0:
                        dve.wait_ge(first_in[j], 64)
                    if m in BANDED_OUT:
                        i = raw[:, slot, :].rearrange("p (A j i) -> p j A i", j=2, i=256)[:, j]
                        o = wt[:, to, :].rearrange("p (k j A b) -> p j A k b", k=KC, j=2, b=32)[:, j]
                    else:
                        i = raw[:, slot, :].rearrange("p (j c i) -> p j c i", j=2, i=256)[:, j]
                        o = wt[:, to, :].rearrange("p (k j c b) -> p j c k b", k=KC, j=2, b=32)[:, j]
                    nc.vector.transpose(o, i).then_inc(wt_ready, 1)

            def compare_keys(g):
                dve.wait_ge(keys_psum, g + 1)
                if g:
                    dve.wait_ge(keys_compared, g)
                for j in range(EG):
                    c = EG * g + j
                    last = nc.vector.scalar_tensor_tensor(
                        out=junk[0:EP, j * EP:(j + 1) * EP], in0=misc[g % 2][0:EP, j * EP:(j + 1) * EP],
                        scalar=edge_work[:, 0, c:c + 1], in1=later[:, :], op0=ALU.is_equal, op1=ALU.mult,
                        accum_out=edge_work[:, 1, c:c + 1])
                last.then_inc(keys_compared, 1)

            def read_latest(g):
                dve.wait_ge(latest_psum, g + 1)
                nc.vector.tensor_reduce(latest_g[:, g, :], misc[2 + g % 2][0:N, 0:EG * N].rearrange(
                    "p (c n) -> p n c", c=EG), AX.X, ALU.max).then_inc(latest_read, 1)

            def build_mask():
                dve.wait_ge(latest_read, EC // EG)
                link(nc.vector.tensor_reduce(latest[:, :], latest_g[:, :, :].rearrange("p g n -> p n g"),
                                             AX.X, ALU.max))
                link(nc.vector.tensor_tensor(latest[:, :], latest[:, :], diag3[:, :], ALU.max))
                link(nc.vector.tensor_copy(latest_i[:, :], latest[:, :]))
                link(nc.vector.tensor_single_scalar(latest_i[:, :], latest_i[:, :], 3, op=ALU.bitwise_and))
                link(nc.vector.tensor_copy(mask_part[:, :], latest_i[:, :]))
                dve.wait_ge(etw_ln, 1)
                nc.vector.scalar_tensor_tensor(out=etw_soft[:, :], in0=etw_all[:, :], scalar=0.0,
                                               in1=etw_a[:, :], op0=ALU.max, op1=ALU.add)
                link(nc.vector.tensor_scalar(mask[:, :], latest[:, :], 2.5, NEG, ALU.is_lt, ALU.mult))
                for w in range(4):
                    link(nc.vector.tensor_scalar(gz[:, 0, :], mask_part[:, :], float(w),
                                                 etw_soft[:, w:w + 1], ALU.is_equal, ALU.mult))
                    ins = nc.vector.tensor_tensor(mask[:, :], mask[:, :], gz[:, 0, :], ALU.add)
                    if w < 3:
                        link(ins)
                    else:
                        ins.then_inc(mask_ready, 1)

            def mask_scores(b):
                dve.wait_ge(scores_psum, b + 1)
                for hh in HEADS_OF[b]:
                    s = slot_of(hh)
                    last = nc.vector.scalar_tensor_tensor(
                        out=probs[:, hh, :], in0=misc[b][0:N, s * N:(s + 1) * N], scalar=SCALE,
                        in1=mask[:, :], op0=ALU.mult, op1=ALU.add)
                link(last)
                heads = probs[:, HEADS_OF[b][0]:HEADS_OF[b][-1] + 1:2, :]
                nc.vector.tensor_reduce(col(NMAX + 4 * b, 4), heads, AX.X, ALU.max, negate=True
                                        ).then_inc(masked_ready, 1)

            def statistics(halves):
                for half in range(2):
                    ins = nc.vector.bn_stats(col(STAT + 6 * half, 6), halves(half))
                link(ins)
                link(nc.vector.bn_aggr(col(AGG, 2), small[0:N, STAT:STAT + 12]))
                nc.vector.tensor_scalar(col(VEPS), col(AGG + 1), EPS, None, ALU.add).then_inc(var_ready, 1)

            dve.wait_ge(x_in, 16)
            nc.vector.tensor_copy(x_band[:, :].rearrange("p (k a d) -> p a k d", k=KC, a=4),
                                  x_nodes[:, :].rearrange("p (a k d) -> p a k d", k=KC, a=4)
                                  ).then_inc(x_band_ready, 1)
            transpose_tile(0)

            def products_with_a(g):
                dve.wait_ge(gat_w_in[g], 64)
                for k in (2 * g, 2 * g + 1):
                    if k:
                        dve.wait_ge(wa_ready, k)
                    nc.vector.scalar_tensor_tensor(
                        out=junk[:, :], in0=gat_w_sb[:, k, :], scalar=1.0, in1=gat_a_all[:, 0, :],
                        op0=ALU.mult, op1=ALU.mult, accum_out=wa[:, 0, k:k + 1]).then_inc(wa_ready, 1)

            def divide_mix(g):
                dve.wait_ge(mix_psum, g + 1)
                to = mixed[:, g * HALF:(g + 1) * HALF].rearrange("p (e f a d) -> p e a f d", e=2, f=2, a=4)
                heads = acc[g][0:N, :].rearrange("p (a e f d) -> p e a f d", a=4, e=2, f=2)
                inv = col(ROWINV + 8 * g, 8).rearrange("p (a e f d) -> p e a f d", a=4, e=2, f=1)
                for e in range(2):
                    nc.vector.tensor_tensor(to[:, e], heads[:, e], inv[:, e].to_broadcast([N, 4, 2, 32]),
                                            ALU.mult).then_inc(mixed_ready, 1)

            def evacuate_oT(g):
                dve.wait_ge(oT_psum, g + 1)
                nc.vector.tensor_tensor(
                    oT[:, 4 * g:4 * g + 4, :], misc[g][:, 0:4 * N].rearrange("p (c n) -> p c n", c=4),
                    biasT[:, 6 * KC + 4 * g:6 * KC + 4 * g + 4].rearrange("p (c n) -> p c n", n=1)
                    .to_broadcast([P, 4, N]), ALU.add).then_inc(oT_ready, 1)

            def residual_1(b):
                dve.wait_ge(tile_done, T_WO + 2 * b + 2)
                for i in range(4):
                    chunk = 4 * (i % 2) + 2 * b + i // 2
                    nc.vector.scalar_tensor_tensor(
                        out=yT[:, chunk, :], in0=misc[2 + b][:, i * N:(i + 1) * N],
                        scalar=biasT[:, 3 * KC + chunk:3 * KC + chunk + 1], in1=xT[:, chunk, :],
                        op0=ALU.add, op1=ALU.add).then_inc(yT_ready, 1)

            def edge_columns():
                dve.wait_ge(etw_in, 16)
                nc.vector.scalar_tensor_tensor(out=etw_a[:, :], in0=etw_all[:, :], scalar=-1.0,
                                               in1=etw_all[:, :], op0=ALU.mult, op1=ALU.min).then_inc(etw_pre, 1)
                dve.wait_ge(edge_psum, 1)
                nc.vector.tensor_copy(edge_cols[:, :, :], misc[3][0:EP, 0:3 * EC].rearrange(
                    "p (k c) -> p k c", k=3)).then_inc(edge_cols_ready, 1)
                dve.wait_ge(edge_cols_ready, 1)
                dve.wait_ge(pool_const, 1)
                nc.vector.scalar_tensor_tensor(out=edge_work[:, 0, :], in0=edge_cols[:, 0, :], scalar=float(N),
                                               in1=edge_cols[:, 1, :], op0=ALU.mult, op1=ALU.add)
                link(nc.vector.tensor_scalar(edge_work[:, 2, :], edge_cols[:, 2, :], 0.0, 4.0, ALU.is_equal,
                                             ALU.mult))
                link(nc.vector.tensor_tensor(edge_work[:, 2, :], edge_work[:, 2, :], edge_cols[:, 2, :], ALU.add))
                link(nc.vector.tensor_tensor(edge_work[:, 3, :], edge_work[:, 2, :], chunk_base[:, :], ALU.add))

            for tile in range(1, TILES):
                transpose_tile(tile)
                if tile == T_WO + 1:
                    dve.wait_ge(probs_ready, HEADS)
                    link(nc.vector.reciprocal(col(ROWINV, HEADS), col(ROWSUM, HEADS)))
                    divide_mix(0)
                    evacuate_oT(0)
                if tile in DOTS_AFTER:
                    if tile == DOTS_AFTER[0]:
                        dve.wait_ge(gat_a_in, 16)
                    products_with_a(DOTS_AFTER.index(tile))
                if tile == 2:
                    edge_columns()
                    dve.wait_ge(xT_ready, 2)
                if 5 <= tile < 9:
                    compare_keys(2 * (tile - 5))
                    compare_keys(2 * (tile - 5) + 1)
                if tile == 8:
                    dve.wait_ge(keys_compared, EC // EG)
                    nc.vector.scalar_tensor_tensor(out=edge_work[:, 4, :], in0=edge_work[:, 1, :],
                                                   scalar=0.5, in1=edge_work[:, 3, :], op0=ALU.is_lt,
                                                   op1=ALU.mult).then_inc(kept_ready, 1)
                if 13 <= tile < 17:
                    read_latest(2 * (tile - 13))
                    read_latest(2 * (tile - 13) + 1)
                if tile == 17:
                    dve.wait_ge(count_psum, 1)
                    nc.vector.tensor_copy(countT[:, :], wide[0][0:N, 0:N]).then_inc(count_ready, 1)
                    dve.wait_ge(count_ready, 1)
                    nc.vector.tensor_scalar(absentT[:, :], countT[:, :], 0.5, NEG, ALU.is_lt, ALU.mult)
                    build_mask()
                    dve.wait_ge(mask_ready, 1)
                if tile == T_WV + 3:
                    for b in range(4):
                        mask_scores(b)
            divide_mix(1)
            evacuate_oT(1)
            products_with_a(2)
            products_with_a(3)
            residual_1(0)
            residual_1(1)
            dve.wait_ge(wa_ready, KC)
            dve.wait_ge(wa1_ready, KC)
            nc.vector.tensor_reduce(wa_sum[:, :], wa[:, :, :], AX.X, ALU.add).then_inc(wa_sum_ready, 1)

            dve.wait_ge(y_psum, 2)
            statistics(lambda half: wide[half][0:N, :])
            nc.vector.tensor_scalar(col(NEGM), col(AGG), -1.0, None, ALU.mult).then_inc(neg_mean_ready, 1)
            dve.wait_ge(dots_psum, 1)
            link(nc.vector.tensor_copy(logit_parts[:, :], misc[0][0:N, 0:4]))
            dve.wait_ge(neg_mean_ready, 1)
            link(nc.vector.scalar_tensor_tensor(out=col(DOTS, 2), in0=logit_parts[:, 2:4], scalar=col(NEGM),
                                                in1=logit_parts[:, 0:2], op0=ALU.mult, op1=ALU.add))
            dve.wait_ge(rstd_ready, 1)
            nc.vector.tensor_scalar(col(AL, 2), col(DOTS, 2), col(RSTD), None, ALU.mult
                                    ).then_inc(logits_ready, 1)
            dve.wait_ge(logits_ready, 1)
            dve.wait_ge(spread_psum, 1)
            link(nc.vector.tensor_scalar(gz[:, 0, :], misc[2][0:N, 0:N], col(AL + 1), None, ALU.add))
            link(nc.vector.scalar_tensor_tensor(out=gz[:, 3, :], in0=gz[:, 0, :], scalar=0.1,
                                                in1=gz[:, 0, :], op0=ALU.mult, op1=ALU.max))
            nc.vector.scalar_tensor_tensor(out=gz[:, 1, :], in0=gz[:, 3, :], scalar=-1.0, in1=absentT[:, :],
                                           op0=ALU.mult, op1=ALU.add).then_inc(gexp_in, 1)
            for half in range(2):
                nc.vector.tensor_scalar(
                    x1[:, :].rearrange("p (a k d) -> p k a d", a=4, k=KC)[:, 4 * half:4 * half + 4],
                    wide[half][0:N, :].rearrange("p (k a d) -> p k a d", k=4, a=4),
                    col(AGG), col(RSTD), ALU.subtract, ALU.mult).then_inc(x1_ready, 1)
            dve.wait_ge(gexp_out, 1)
            nc.vector.tensor_tensor(gz[:, 4, :], gz[:, 2, :], countT[:, :], ALU.mult).then_inc(adj_ready, 1)
            dve.wait_ge(degree_psum, 1)
            link(nc.vector.tensor_scalar(col(INV + 1), misc[3][0:N, 0:1], EPS, None, ALU.add))
            nc.vector.reciprocal(col(INV), col(INV + 1)).then_inc(inv_ready, 1)

            def y2_half(half):
                return y2[:, half * HALF:(half + 1) * HALF]

            def residual_2(half):
                dve.wait_ge(elu_done, 2 * half + 1)
                span = slice(half * HALF, (half + 1) * HALF)
                link(nc.vector.scalar_tensor_tensor(out=y2_half(half), in0=elu_e[:, span], scalar=1.0,
                                                    in1=x1[:, span], op0=ALU.min, op1=ALU.add))
                dve.wait_ge(elu_done, 2 * half + 2)
                link(nc.vector.scalar_tensor_tensor(out=y2_half(half), in0=elu_r[:, span], scalar=-1.0,
                                                    in1=y2_half(half), op0=ALU.add, op1=ALU.add))
                return y2_half(half)

            dve.wait_ge(x1_ready, 2)
            statistics(residual_2)
            dve.wait_ge(rstd_ready, 2)
            for half in range(2):
                span = slice(half * HALF, (half + 1) * HALF)
                nc.vector.tensor_scalar(final[:, span], y2_half(half), col(AGG), col(RSTD), ALU.subtract,
                                        ALU.mult).then_inc(final_ready, 1)

        @block.tensor
        def _(pe):
            pe.wait_ge(ident_ready, 1)
            for _ in range(WARM_UP):
                nc.tensor.matmul(misc[3][:, 0:P], ident[:, :], ident[:, :], start=True, stop=True)
            pe.wait_ge(x_band_ready, 1)
            for k in range(KC):
                last = nc.tensor.transpose(misc[k // 4][:, (k % 4) * N:(k % 4 + 1) * N], x_band[:, k * P:(k + 1) * P],
                                           ident[0:N, 0:N])
                if k % 4 == 3:
                    last.then_inc(xT_psum, 1)
            def transpose_biases():
                pe.wait_ge(bias_in, 16 * 8)
                nc.tensor.transpose(misc[2][:, 0:NB * KC], bias_rows[:, :], ident[0:NB * KC, 0:NB * KC]
                                    ).then_inc(bias_psum, 1)

            def transpose_edges():
                pe.wait_ge(edge_conv, 1)
                for k in range(3):
                    last = nc.tensor.transpose(misc[3][0:EP, k * EC:(k + 1) * EC], edge_rows[:, k, :],
                                               ident[0:EC, 0:EC])
                last.then_inc(edge_psum, 1)

            def column_products(tile, rhs):
                turn = tile
                m, slot = matrix_of(tile), tile % NWT
                if turn >= 2:
                    pe.wait_ge(acc_read, turn - 1)
                for j in range(2):
                    pe.wait_ge(wt_ready, 2 * tile + j + 1)
                    for k in range(KC):
                        last = nc.tensor.matmul(acc[turn % 2][:, j * N:(j + 1) * N],
                                                wt[:, slot, k * TR + j * P:k * TR + (j + 1) * P],
                                                rhs[:, k, :], start=(k == 0), stop=(k == KC - 1))
                last.then_inc(tile_done, 1)

            def row_products(tile, part):
                slot, t = tile % NWT, tile % TPM
                pe.wait_ge(wt_ready, 2 * tile + 2)
                order = (0, 4, 1, 5, 2, 6, 3, 7)
                for i in range(4 * part, 4 * part + 4):
                    k = order[i]
                    if tile == T_WIV and i % 2 == 0:
                        pe.wait_ge(acc_read, T_WV + i // 2 + 1)
                    last = nc.tensor.matmul(wide[t // 2][0:N, (t % 2) * TR:(t % 2 + 1) * TR],
                                            vT[:, k, :], wt[:, slot, k * TR:(k + 1) * TR],
                                            start=(i == 0), stop=(i == KC - 1))
                if part == 1:
                    last.then_inc(tile_done, 1)

            def spread_keys(g):
                if g >= 2:
                    pe.wait_ge(keys_compared, g - 1)
                span = slice(g * EG * EP, (g + 1) * EG * EP)
                nc.tensor.matmul(misc[g % 2][0:EP, 0:EG * EP], times_n[:, :], key_src[:, span],
                                 start=True, stop=False)
                nc.tensor.matmul(misc[g % 2][0:EP, 0:EG * EP], times_1[:, :], key_dst[:, span],
                                 start=False, stop=True).then_inc(keys_psum, 1)

            def latest_edges(g):
                if g >= 2:
                    pe.wait_ge(latest_read, g - 1)
                for j in range(EG):
                    last = nc.tensor.matmul(misc[2 + g % 2][0:N, j * N:(j + 1) * N], src_hot[:, EG * g + j, :],
                                            dst_val[:, EG * g + j, :], start=True, stop=True)
                last.then_inc(latest_psum, 1)

            sources = {T_WQ: xT, T_WK: xT, T_WIQ: qT, T_WIK: kT, T_WV: xT}
            pe.wait_ge(xT_ready, 2)
            for tile in range(T_WIV):
                if tile == T_WIQ:
                    pe.wait_ge(acc_read, T_WK)
                if tile == T_WIK:
                    pe.wait_ge(acc_read, T_WIQ)
                column_products(tile, sources[matrix_of(tile)])
                if tile == 0:
                    transpose_biases()
                if tile == 1:
                    transpose_edges()
                if tile == 3:
                    pe.wait_ge(keys_placed, 2)
                    pe.wait_ge(pool_const, 1)
                if 3 <= tile < 7:
                    spread_keys(2 * (tile - 3))
                    spread_keys(2 * (tile - 3) + 1)
                if tile == 11:
                    pe.wait_ge(val_ready, 1)
                    pe.wait_ge(hot_ready, 2)
                if 11 <= tile < 15:
                    latest_edges(2 * (tile - 11))
                    latest_edges(2 * (tile - 11) + 1)
                if tile == T_WV - 1:
                    for c in range(EC):
                        last = nc.tensor.matmul(wide[0][0:N, 0:N], dst_hot[:, c, :], src_hot[:, c, :],
                                                start=(c == 0), stop=(c == EC - 1))
                    last.then_inc(count_psum, 1)
                if tile == T_WV:
                    pe.wait_ge(acc_read, T_WV)
                    pe.wait_ge(keys_compared, EC // EG)
                    pe.wait_ge(latest_read, EC // EG)
                    for b in range(4):
                        for hh in HEADS_OF[b]:
                            rows = slice(HD * (hh % 2), HD * (hh % 2) + HD)
                            last = nc.tensor.matmul(misc[b][0:N, slot_of(hh) * N:(slot_of(hh) + 1) * N],
                                                    q2T[rows, hh // 2, :], k2T[rows, hh // 2, :],
                                                    start=True, stop=True)
                        last.then_inc(scores_psum, 1)
            pe.wait_ge(count_ready, 1)

            def mix_heads(g):
                pe.wait_ge(wide_read, g + 1)
                for hh in range(8 * g, 8 * g + 8):
                    last = nc.tensor.matmul(acc[g][0:N, (hh % 8) * HD:(hh % 8 + 1) * HD],
                                            probsT[:, 4 * bank_of(hh) + slot_of(hh), :],
                                            v2[:, hh * HD:(hh + 1) * HD], start=True, stop=True)
                last.then_inc(mix_psum, 1)

            def transpose_mixed(g):
                pe.wait_ge(mixed_ready, 2 * g + 2)
                for k in range(4):
                    last = nc.tensor.transpose(misc[g][:, k * N:(k + 1) * N],
                                               mixed[:, (4 * g + k) * P:(4 * g + k + 1) * P],
                                               ident[0:N, 0:N])
                last.then_inc(oT_psum, 1)

            def project(t, g, js):
                tile = T_WO + t
                if g == 0:
                    pe.wait_ge(wt_ready, 2 * tile + 2)
                for j in js:
                    i = 2 * (t % 2) + j
                    for k in range(4 * g, 4 * g + 4):
                        at = k * TR + j * P
                        last = nc.tensor.matmul(misc[2 + t // 2][:, i * N:(i + 1) * N],
                                                wt[:, tile % NWT, at:at + P], oT[:, k, :],
                                                start=(i == 0 and k == 0), stop=(k == KC - 1),
                                                skip_group_check=True)
                if g == 1:
                    last.then_inc(tile_done, 1)

            row_products(T_WIV, 0)
            row_products(T_WIV, 1)
            pe.wait_ge(masked_ready, 4)
            for b in range(4):
                for hh in HEADS_OF[b]:
                    pe.wait_ge(probs_ready, HEAD_ORDER.index(hh) + 1)
                    last = nc.tensor.transpose(misc[b][0:N, slot_of(hh) * N:(slot_of(hh) + 1) * N],
                                               probs[:, hh, :], ident[0:N, 0:N])
                last.then_inc(probsT_psum, 1)
            for tile in (T_WIV + 1, T_WIV + 2):
                row_products(tile, 0)
                row_products(tile, 1)
            pe.wait_ge(probsT_ready, 4)
            mix_heads(0)
            row_products(T_WIV + 3, 0)
            transpose_mixed(0)
            row_products(T_WIV + 3, 1)
            pe.wait_ge(oT_ready, 1)
            project(0, 0, (0, 1))
            mix_heads(1)
            project(1, 0, (0, 1))
            project(2, 0, (0, 1))
            project(3, 0, (0,))
            transpose_mixed(1)
            project(3, 0, (1,))
            pe.wait_ge(oT_ready, 2)
            for t in range(TPM):
                project(t, 1, (0, 1))

            def graph_products(half, ks, start=False):
                for k in ks:
                    nc.tensor.matmul(acc[half][0:N, :], yT[:, k, :],
                                     gat_w_sb[:, k, half * HALF:(half + 1) * HALF],
                                     start=(start and k == ks[0]), stop=False)

            def subtract_mean(half):
                nc.tensor.matmul(acc[half][0:N, :], mean_rows[:, :], wsum[:, half * HALF:(half + 1) * HALF],
                                 start=False, stop=True).then_inc(h_psum, 1)

            for g in range(4):
                pe.wait_ge(gat_w_in[g], 64)
            pe.wait_ge(yT_ready, 4)
            graph_products(0, (0, 4, 1, 5), start=True)
            pe.wait_ge(yT_ready, 8)
            for k in range(KC):
                last = nc.tensor.transpose(wide[k // 4][0:N, (k % 4) * P:(k % 4 + 1) * P], yT[:, k, :],
                                           ident[:, :])
                if k % 4 == 3:
                    last.then_inc(y_psum, 1)
            graph_products(0, (2, 6, 3, 7))
            pe.wait_ge(wa_sum_ready, 1)
            nc.tensor.matmul(misc[0][0:N, 2:4], ones[:, :], wa_sum[:, :], start=True, stop=True)
            for k in range(KC):
                last = nc.tensor.matmul(misc[0][0:N, 0:2], yT[:, k, :],
                                        wa[:, :, k], start=(k == 0), stop=(k == KC - 1))
            last.then_inc(dots_psum, 1)
            pe.wait_ge(neg_mean_ready, 1)
            nc.tensor.matmul(misc[1][:, 0:N], col(NEGM).to_broadcast([N, P]), ident[0:N, 0:N],
                             start=True, stop=True).then_inc(mean_psum, 1)
            graph_products(1, (0, 1), start=True)
            pe.wait_ge(logits_ready, 1)
            nc.tensor.matmul(misc[2][0:N, 0:N], col(AL).to_broadcast([N, N]), ident[0:N, 0:N],
                             start=True, stop=True).then_inc(spread_psum, 1)
            pe.wait_ge(mean_rows_ready, 1)
            pe.wait_ge(wsum_ready, 1)
            subtract_mean(0)
            graph_products(1, (2, 3, 4))

            def aggregate(half):
                pe.wait_ge(h_ready, half + 1)
                nc.tensor.matmul(wide[half][0:N, :], gz[:, 4, :], h[:, half * HALF:(half + 1) * HALF],
                                 start=True, stop=True).then_inc(agg_psum, 1)

            pe.wait_ge(adj_ready, 1)
            nc.tensor.matmul(misc[3][0:N, 0:1], gz[:, 4, :], ones[0:N, 0:1], start=True, stop=True
                             ).then_inc(degree_psum, 1)
            pe.wait_ge(x1_ready, 2)
            aggregate(0)
            graph_products(1, (5, 6, 7))
            subtract_mean(1)
            aggregate(1)


_INS = ['x', 'src', 'dst', 'edge_type_5', 'L0_gnn_edge_type_weights', 'L0_gnn_wq', 'L0_gnn_bq', 'L0_gnn_wk',
        'L0_gnn_bk', 'L0_gnn_wv', 'L0_gnn_bv', 'L0_gnn_wiq', 'L0_gnn_biq', 'L0_gnn_wik', 'L0_gnn_bik',
        'L0_gnn_wiv', 'L0_gnn_biv', 'L0_gnn_wo', 'L0_gnn_bo', 'L1_gnn_W', 'L1_gnn_a']


def kernel(**inputs):
    import numpy as _np
    import concourse.bacc as _bacc
    from concourse import mybir as _mybir
    from concourse.bass_utils import run_bass_kernel_spmd as _run

    nc = _bacc.Bacc("TRN2", target_bir_lowering=False, num_devices=1)
    arrays, args = {}, []
    for name in _INS:
        a = _np.ascontiguousarray(inputs[name])
        arrays[f"in_{name}"] = a
        args.append(nc.dram_tensor(f"in_{name}", a.shape, _mybir.dt.from_np(a.dtype), kind="ExternalInput").ap())
    out = nc.dram_tensor("out_0", (96, 1024), _mybir.dt.float32, kind="ExternalOutput").ap()
    build(nc, *args, out)
    r = _run(nc, [arrays], core_ids=[0])
    return r.results[0]["out_0"]
```

```python
import concourse.bass as bass
from concourse import mybir
from contextlib import ExitStack


def build(nc, x, src, dst, edge_type_5, etw, wq, bq, wk, bk, wv, bv, wiq, biq, wik, bik, wiv, biv, wo, bo,
          gat_w, gat_a, out):
    f32, bf16, i32 = mybir.dt.float32, mybir.dt.bfloat16, mybir.dt.int32
    ALU, ACT, AX = mybir.AluOpType, mybir.ActivationFunctionType, mybir.AxisListType

    N, F = x.shape
    P = 128
    KC = F // P
    HEADS, HD = 16, F // 16
    HALF = F // 2
    SCALE = HD ** -0.5
    EC = 32
    EP = src.shape[0] // EC
    EG = 4
    WARM_UP = (8, 4)
    NEG = -1.0e30
    EPS = 1e-5

    TR = 256
    TPM = F // TR
    NRAW, NWT = 6, 6
    STREAM = [wq, wk, wiq, wik, wv, wiv, wo]
    TILES = TPM * len(STREAM)
    T_WQ, T_WK, T_WIQ, T_WIK, T_WV, T_WIV, T_WO = [TPM * m for m in range(7)]
    BANDED_OUT = (T_WQ, T_WK, T_WV, T_WO)

    GAT_W_AFTER = (T_WIV + 1, T_WIV + 3, T_WO + 1, T_WO + 3)

    HALVED_LOADS = 1

    def matrix_of(tile):
        return tile - tile % TPM

    ctx = ExitStack()
    with ctx:
        def sb(name, shape, dt=f32):
            return ctx.enter_context(nc.sbuf_tensor(name, shape, dt))

        def ps(name):
            return ctx.enter_context(nc.psum_tensor(name, [P, 512], f32))

        def sem(name):
            return ctx.enter_context(nc.semaphore(name))

        raw = sb("raw", [P, NRAW, KC * TR])
        wt = sb("wt", [P, NWT, KC * TR])
        gat_w_sb = sb("gat_w_sb", [P, KC, 2 + F])
        x_nodes = sb("x_nodes", [N, F])
        scratch = sb("scratch", [P, F])
        xT = sb("xT", [P, KC, N])
        qT = sb("qT", [P, KC, N])
        kT = sb("kT", [P, KC, N])
        vT = sb("vT", [P, KC, N])
        q2T = sb("q2T", [P, KC, N])
        k2T = sb("k2T", [P, KC, N])
        v2 = sb("v2", [N, F])
        probs = sb("probs", [N, HEADS, N])
        probsT = sb("probsT", [N, HEADS, N])
        mixed = sb("mixed", [N, F])
        gat_a_all = sb("gat_a_all", [P, 2, F])
        wsum = sb("wsum", [P, F])
        wa_sum = sb("wa_sum", [P, 2])
        wa_prod = sb("wa_prod", [P, F])
        ones = sb("ones", [P, N])
        mean_rows = sb("mean_rows", [P, N])
        logit_parts = sb("logit_parts", [N, 4])
        ident = sb("ident", [P, P])
        NB = 7
        bias_rows = sb("bias_rows", [NB * KC, P])
        biasT = sb("biasT", [P, NB * KC])
        small = sb("small", [P, 256])
        edge_rows_i = sb("edge_rows_i", [2 * EC, 3, EP], i32)
        edge_rows = sb("edge_rows", [2 * EC, 3, EP])
        edge_cols = sb("edge_cols", [EP, 3, EC])
        edge_work = sb("edge_work", [EP, 5, EC])
        key_weights = sb("key_weights", [2 * EC, EP], bf16)
        own_chunk = sb("own_chunk", [2 * EC, EC])
        later = sb("later", [EP, EP])
        node_ids = sb("node_ids", [EP, N])
        chunk_base = sb("chunk_base", [EP, EC])
        diag3 = sb("diag3", [N, N])
        latest_g = sb("latest_g", [N, EC // EG, N])
        latest = sb("latest", [N, N])
        latest_i = sb("latest_i", [N, N], i32)
        mask = sb("mask", [N, N])
        mask_part = sb("mask_part", [N, N])
        countT = sb("countT", [N, N])
        absentT = sb("absentT", [N, N])
        etw_all = sb("etw_all", [N, 4])
        etw_a = sb("etw_a", [N, 4])
        etw_soft = sb("etw_soft", [N, 4])
        weight_term = sb("weight_term", [N, N])
        z_sum = sb("z_sum", [N, N])
        z_leaky = sb("z_leaky", [N, N])
        z_masked = sb("z_masked", [N, N])
        z_exp = sb("z_exp", [N, N])
        attention = sb("attention", [N, N])
        wa = gat_w_sb[:, :, 0:2]
        w_cols = gat_w_sb[:, :, 2:2 + F]
        region = gat_w_sb[:, :, :].rearrange("p k n -> p (k n)").bitcast(bf16)
        key_rows = region[0:2 * EC, 0:EC * EP]
        at = EC * EP
        src_hot = region[0:EP, at:at + EC * N].rearrange("p (c n) -> p c n", c=EC)
        dst_hot = region[0:EP, at + EC * N:at + 2 * EC * N].rearrange("p (c n) -> p c n", c=EC)
        dst_val = region[0:EP, at + 2 * EC * N:at + 3 * EC * N].rearrange("p (c n) -> p c n", c=EC)

        x_band = scratch[0:N, :]
        junk = scratch
        oT = qT
        yT = vT
        x1 = x_nodes
        x1_banded = scratch[0:N, :]
        sumsT = kT
        h = v2
        elu_e = mixed
        elu_r = gat_a_all[0:N, 0, :]
        y2 = probs[:, :, :].rearrange("p h n -> p (h n)")[:, 0:F]
        final = probsT[:, :, :].rearrange("p h n -> p (h n)")[:, 0:F]

        acc = [ps(f"acc{i}") for i in range(2)]
        wide = [ps(f"wide{i}") for i in range(2)]
        misc = [ps(f"misc{i}") for i in range(4)]
        z_banks = (wide[0], wide[1], misc[3], misc[2])
        sums_banks = (misc[0], misc[3])

        raw_in = [sem(f"raw_in{i}") for i in range(NRAW)]
        x_in, bias_in, natural_in = sem("x_in"), sem("bias_in"), sem("natural_in")
        edge_in, edge_low_in, etw_in = sem("edge_in"), sem("edge_low_in"), sem("etw_in")
        first_in = [[sem(f"first_in{tile}{j}") for j in range(2)] for tile in range(HALVED_LOADS)]
        gat_w_in = [sem(f"gat_w_in{g}") for g in range(4)]
        gat_a_in, out_done = sem("gat_a_in"), sem("out_done")
        wt_ready, tile_done = sem("wt_ready"), sem("tile_done")
        acc_read, wide_read = sem("acc_read"), sem("wide_read")
        x_band_ready = sem("x_band_ready")
        ident_ready, xT_psum, xT_ready, bias_psum, bias_ready = (
            sem("ident_ready"), sem("xT_psum"), sem("xT_ready"), sem("bias_psum"), sem("bias_ready"))
        pool_const, edge_conv, edge_psum, edge_cols_ready, keys_placed = (
            sem("pool_const"), sem("edge_conv"), sem("edge_psum"), sem("edge_cols_ready"), sem("keys_placed"))
        keys_psum, keys_compared, kept_ready, hot_ready, val_ready = (
            sem("keys_psum"), sem("keys_compared"), sem("kept_ready"), sem("hot_ready"), sem("val_ready"))
        latest_psum, latest_read, count_psum, count_ready = (
            sem("latest_psum"), sem("latest_read"), sem("count_psum"), sem("count_ready"))
        etw_pre, etw_ln, mask_ready = sem("etw_pre"), sem("etw_ln"), sem("mask_ready")
        scores_psum, masked_ready, probs_ready, probsT_psum, probsT_ready = (
            sem("scores_psum"), sem("masked_ready"), sem("probs_ready"), sem("probsT_psum"),
            sem("probsT_ready"))
        mix_psum, mixed_ready, oT_psum, oT_ready = (
            sem("mix_psum"), sem("mixed_ready"), sem("oT_psum"), sem("oT_ready"))
        yT_ready, y_psum, var_ready, x1_ready = (
            sem("yT_ready"), sem("y_psum"), sem("var_ready"), sem("x1_ready"))
        wsum_ready, wa_ready, wa_sum_ready, neg_mean_ready, mean_psum, mean_rows_ready, rstd_ready = (
            sem("wsum_ready"), sem("wa_ready"), sem("wa_sum_ready"), sem("neg_mean_ready"),
            sem("mean_psum"), sem("mean_rows_ready"), sem("rstd_ready"))
        h_psum, h_ready, dots_psum, logits_ready, spread_psum, gexp_in, gexp_out, adj_ready = (
            sem("h_psum"), sem("h_ready"), sem("dots_psum"), sem("logits_ready"), sem("spread_psum"),
            sem("gexp_in"), sem("gexp_out"), sem("adj_ready"))
        wa_prod_ready, wa1_ready = sem("wa_prod_ready"), sem("wa1_ready")
        agg_psum, degree_psum, x1_back = sem("agg_psum"), sem("degree_psum"), sem("x1_back")
        sums_psum, sums_ready = sem("sums_psum"), sem("sums_ready")
        inv_ready, elu_done, final_ready = sem("inv_ready"), sem("elu_done"), sem("final_ready")
        pool_chain, dve_chain, act_chain = sem("pool_chain"), sem("dve_chain"), sem("act_chain")

        AGG, VEPS, RSTD, NEGM, MHALF, STAT = 0, 2, 3, 4, 5, 96
        ROWSUM, ROWINV, NMAX, DOTS, AL, INV = 32, 48, 64, 80, 84, 86

        def col(c, w=1, p=N):
            return small[0:p, c:c + w]

        PIECES = (slice(0, 3 * P), slice(3 * P, 5 * P), slice(5 * P, 7 * P), slice(7 * P, F))

        OUT_PARTS = (slice(0, 5 * P), slice(5 * P, F))
        SPLIT = TR - 2
        PARTS = (slice(0, SPLIT), slice(SPLIT, PIECES[0].stop))

        def width(piece):
            return PIECES[piece].stop - PIECES[piece].start

        def bank_of(head):
            return (head % 2) * 2 + head // 8

        def slot_of(head):
            return (head // 2) % 4

        HEADS_OF = [[hh for hh in range(HEADS) if bank_of(hh) == b] for b in range(4)]
        HEAD_ORDER = [hh for b in range(4) for hh in HEADS_OF[b]]

        def quarter(t, n):
            return t[0:N, 0:4 * n].rearrange("p (c n) -> p c n", c=4)

        block = ctx.enter_context(nc.Block())

        @block.sync
        def _(sp):
            def load_tile(tile):
                m, t, slot = matrix_of(tile), tile % TPM, tile % NRAW
                w = STREAM[tile // TPM]
                if m in BANDED_OUT:
                    rows = w.rearrange("(c t b) i -> t b c i", c=8, t=TPM, b=32)[t]
                else:
                    rows = w.rearrange("(t c b) i -> t b c i", c=8, t=TPM, b=32)[t]
                if tile >= NRAW:
                    sp.wait_ge(wt_ready, 2 * (tile - NRAW + 1))
                for a in range(4):
                    to = raw[32 * a:32 * a + 32, slot, :].rearrange("p (c i) -> p c i", c=8)
                    if m == T_WO:
                        for g in range(2):
                            i0 = 512 * g + 128 * a
                            sp.dma_start(to[:, :, 128 * g:128 * g + 128], rows[:, :, i0:i0 + 128]
                                         ).then_inc(raw_in[slot], 16)
                    else:
                        sp.dma_start(to, rows[:, :, 256 * a:256 * a + 256]).then_inc(raw_in[slot], 16)

            def load_tile_halves(tile):
                rows = wq.rearrange("(A j t b) i -> t j b A i", A=4, j=2, t=TPM, b=32)[tile]
                for j in range(2):
                    for a in range(4):
                        to = raw[32 * a:32 * a + 32, tile, :].rearrange("p (A j i) -> p j A i", A=4, j=2)
                        sp.dma_start(to[:, j], rows[j, :, :, 256 * a:256 * a + 256]
                                     ).then_inc(first_in[tile][j], 16)

            def load_gat_w(g):
                if g == 0:
                    sp.wait_ge(count_psum, 1)
                    sp.wait_ge(latest_psum, EC // EG)
                gw = gat_w.rearrange("(a k b) n -> a b k n", a=4, k=KC)
                for a in range(4):
                    sp.dma_start(w_cols[32 * a:32 * a + 32, 2 * g:2 * g + 2, :],
                                 gw[a, :, 2 * g:2 * g + 2, :]).then_inc(gat_w_in[g], 16)

            sp.dma_start(x_nodes[:, :], x).then_inc(x_in, 16)
            for tile in range(HALVED_LOADS):
                load_tile_halves(tile)
            for tile in range(HALVED_LOADS, TILES):
                load_tile(tile)
                if tile in GAT_W_AFTER:
                    load_gat_w(GAT_W_AFTER.index(tile))
            for half in range(2):
                sp.wait_ge(final_ready, half + 1)
                cols = OUT_PARTS[half]
                sp.dma_start(out[:, cols], final[:, cols]).then_inc(out_done, 16)
            sp.wait_ge(out_done, 32)

        @block.gpsimd
        def _(pool):
            links = [0]

            def link(ins):
                links[0] += 1
                ins.then_inc(pool_chain, 1)
                pool.wait_ge(pool_chain, links[0])

            link(nc.gpsimd.memset(ident[:, :], 0.0))
            nc.gpsimd.affine_select(out=ident[:, :], in_=ident[:, :], compare_op=ALU.not_equal, fill=1.0,
                                    base=0, pattern=[[-1, P]], channel_multiplier=1).then_inc(ident_ready, 1)
            for m, b in enumerate((bq, bk, bv, bo)):
                pool.dma_start(bias_rows[KC * m:KC * m + KC, :].rearrange("k (a d) -> k a d", a=4),
                               b.rearrange("(a k d) -> k a d", a=4, k=KC)).then_inc(bias_in, 16)
            pool.dma_start(bias_rows[KC * 5:KC * 6, :], bik.rearrange("(k p) -> k p", p=P)
                           ).then_inc(bias_in, 16)
            for g in range(2):
                pool.dma_start(bias_rows[KC * 6 + 4 * g:KC * 6 + 4 * g + 4, :]
                               .rearrange("k (a d) -> k a d", a=4),
                               biv.rearrange("(g a k d) -> g k a d", g=2, a=4, k=4)[g]
                               ).then_inc(bias_in, 16)
            pool.dma_start(etw_all[:, :], etw.rearrange("(o n) -> o n", o=1).to_broadcast([N, 4])
                           ).then_inc(etw_in, 16)
            link(nc.gpsimd.memset(later[:, :], 1.0))
            link(nc.gpsimd.memset(diag3[:, :], 0.0))
            nc.gpsimd.memset(ones[:, :], 1.0)
            nc.gpsimd.memset(small[:, MHALF:MHALF + 1], -0.5)
            link(nc.gpsimd.memset(key_weights[:, :], 1.0))
            nc.gpsimd.memset(key_weights[0:EC, :], float(N))
            nc.gpsimd.tensor_tensor(own_chunk[:, :], ident[0:2 * EC, 0:EC], ident[0:2 * EC, EC:2 * EC], ALU.add)
            nc.gpsimd.iota(node_ids[:, :], pattern=[[1, N]], base=0, channel_multiplier=0,
                           allow_small_or_imprecise_dtypes=True)
            nc.gpsimd.iota(chunk_base[:, :], pattern=[[4, EC]], base=3, channel_multiplier=0,
                           allow_small_or_imprecise_dtypes=True)
            nc.gpsimd.affine_select(out=later[:, :], in_=later[:, :], compare_op=ALU.is_gt, fill=0.0,
                                    base=0, pattern=[[1, EP]], channel_multiplier=-1)
            nc.gpsimd.affine_select(out=diag3[:, :], in_=diag3[:, :], compare_op=ALU.not_equal, fill=3.0,
                                    base=0, pattern=[[-1, N]], channel_multiplier=1).then_inc(pool_const, 1)
            pool.wait_ge(edge_in, 48)
            nc.gpsimd.tensor_copy(edge_rows[0:EC, :, :], edge_rows_i[0:EC, :, :]).then_inc(edge_conv, 1)
            pool.wait_ge(edge_conv, 1)
            pool.wait_ge(edge_low_in, 16)
            nc.gpsimd.tensor_copy(edge_rows[EC:2 * EC, 0, :], edge_rows_i[EC:2 * EC, 0, :]).then_inc(edge_conv, 1)
            pool.wait_ge(edge_conv, 2)
            pool.wait_ge(pool_const, 1)
            nc.gpsimd.tensor_tensor(key_rows.rearrange("p (c e) -> p c e", c=EC),
                                    edge_rows[:, 0:1, :].to_broadcast([2 * EC, EC, EP]),
                                    own_chunk[:, :].rearrange("p (c e) -> p c e", e=1)
                                    .to_broadcast([2 * EC, EC, EP]), ALU.mult).then_inc(keys_placed, 1)
            pool.wait_ge(edge_cols_ready, 1)
            for k, hot in enumerate((src_hot, dst_hot)):
                link(nc.gpsimd.tensor_tensor(hot, node_ids[:, :].rearrange("p (c n) -> p c n", c=1)
                                        .to_broadcast([EP, EC, N]),
                                        edge_cols[:, k, :].rearrange("p (c n) -> p c n", n=1)
                                        .to_broadcast([EP, EC, N]), ALU.subtract))
                nc.gpsimd.tensor_scalar(hot, hot, 0.0, None, ALU.is_equal).then_inc(hot_ready, 1)
            pool.wait_ge(hot_ready, 2)
            pool.wait_ge(kept_ready, 1)
            nc.gpsimd.tensor_tensor(dst_val, dst_hot,
                                    edge_work[:, 4, :].rearrange("p (c n) -> p c n", n=1)
                                    .to_broadcast([EP, EC, N]), ALU.mult).then_inc(val_ready, 1)
            pool.dma_start(gat_a_all[:, :, :].rearrange("p a n -> p (a n)"), gat_a.to_broadcast([P, 2 * F])
                           ).then_inc(gat_a_in, 16)
            pool.wait_ge(gat_a_in, 16)
            for g in range(4):
                pool.wait_ge(gat_w_in[g], 64)
                for k in (2 * g, 2 * g + 1):
                    if k:
                        pool.wait_ge(wa1_ready, k)
                    nc.gpsimd.tensor_tensor(wa_prod[:, :], w_cols[:, k, :], gat_a_all[:, 1, :], ALU.mult
                                            ).then_inc(wa_prod_ready, 1)
                    if k == 0:
                        continue
                    first = w_cols[:, 0, :] if k == 1 else wsum[:, :]
                    ins = nc.gpsimd.tensor_tensor(wsum[:, :], first, w_cols[:, k, :], ALU.add)
                    if k < KC - 1:
                        link(ins)
                    else:
                        ins.then_inc(wsum_ready, 1)
            for turn in range(2):
                pool.wait_ge(var_ready, turn + 1)
                nc.gpsimd.tensor_tensor(col(RSTD), col(VEPS), col(MHALF), ALU.pow).then_inc(rstd_ready, 1)

        @block.scalar
        def _(act):
            links = [0]

            def link(ins):
                links[0] += 1
                ins.then_inc(act_chain, 1)
                act.wait_ge(act_chain, links[0])

            nc.scalar.preload_act_table_set("natural_log_exp_and_others")
            for g in range(2):
                act.wait_ge(xT_psum, g + 1)
                nc.scalar.activation(xT[:, 4 * g:4 * g + 4, :], misc[g][:, 0:4 * N].rearrange(
                    "p (c n) -> p c n", c=4), ACT.Copy).then_inc(xT_ready, 1)
            act.dma_start(bias_rows[KC * 4:KC * 5, :], biq.rearrange("(k p) -> k p", p=P)
                          ).then_inc(natural_in, 16)
            for k, e in enumerate((src, dst, edge_type_5)):
                act.dma_start(edge_rows_i[0:EC, k, :], e.rearrange("(c e) -> c e", c=EC)).then_inc(edge_in, 16)
            act.dma_start(edge_rows_i[EC:2 * EC, 0, :], dst.rearrange("(c e) -> c e", c=EC)
                          ).then_inc(edge_low_in, 16)
            act.wait_ge(bias_psum, 1)
            nc.scalar.activation(biasT[:, :], misc[2][:, 0:NB * KC], ACT.Copy).then_inc(bias_ready, 1)
            act.wait_ge(bias_ready, 1)

            dest = {T_WQ: (qT, 0), T_WK: (kT, 1), T_WIQ: (q2T, 4), T_WIK: (k2T, 5), T_WV: (vT, 2)}

            def evacuate(tile, turn):
                act.wait_ge(tile_done, tile + 1)
                m, t = matrix_of(tile), tile % TPM
                to, brow = dest[m]
                for j in range(2):
                    chunk = 4 * j + t if m in BANDED_OUT else 2 * t + j
                    last = nc.scalar.activation(to[:, chunk, :], acc[turn % 2][:, j * N:(j + 1) * N],
                                                ACT.Identity,
                                                bias=biasT[:, KC * brow + chunk:KC * brow + chunk + 1])
                last.then_inc(acc_read, 1)

            def exps(b):
                act.wait_ge(masked_ready, b + 1)
                for hh in HEADS_OF[b]:
                    nc.scalar.activation(probs[:, hh, :], probs[:, hh, :], ACT.Exp,
                                         bias=col(NMAX + 4 * b + slot_of(hh)),
                                         accum_out=col(ROWSUM + hh)).then_inc(probs_ready, 1)

            def add_up(k):
                act.wait_ge(wa_prod_ready, k + 1)
                nc.scalar.activation(wa_prod[:, :], wa_prod[:, :], ACT.Copy, accum_out=wa[:, k, 1:2]
                                     ).then_inc(wa1_ready, 1)

            for tile in range(T_WIV):
                evacuate(tile, tile)
                if tile == TPM:
                    act.wait_ge(etw_pre, 1)
                    link(nc.scalar.activation(etw_a[:, :], etw_a[:, :], ACT.Exp))
                    nc.scalar.activation(etw_a[:, :], etw_a[:, :], ACT.Ln, bias=1.0).then_inc(etw_ln, 1)
                if tile == T_WV + 1:
                    add_up(0)
                if tile > T_WV:
                    exps(tile - T_WV - 1)
            exps(3)
            add_up(1)
            for b in range(4):
                act.wait_ge(probsT_psum, b + 1)
                nc.scalar.activation(probsT[:, 4 * b:4 * b + 4, :], quarter(misc[b], N), ACT.Copy
                                     ).then_inc(probsT_ready, 1)
            add_up(2)
            for half in range(2):
                act.wait_ge(tile_done, T_WIV + 2 * half + 2)
                nc.scalar.activation(v2[:, half * HALF:(half + 1) * HALF], wide[half][0:N, :], ACT.Copy
                                     ).then_inc(wide_read, 1)
                add_up(3 + half)
            for k in range(5, KC):
                add_up(k)
            act.wait_ge(mean_psum, 1)
            nc.scalar.activation(mean_rows[:, :], misc[1][:, 0:N], ACT.Copy).then_inc(mean_rows_ready, 1)
            act.wait_ge(rstd_ready, 1)

            def elu_parts(piece):
                act.wait_ge(agg_psum, piece + 1)
                cols = PIECES[piece]
                nc.scalar.activation(elu_e[:, cols], z_banks[piece][0:N, 0:width(piece)], ACT.Exp, scale=col(INV)
                                     ).then_inc(elu_done, 1)
                nc.scalar.activation(elu_r[:, cols], z_banks[piece][0:N, 0:width(piece)], ACT.Relu, scale=col(INV)
                                     ).then_inc(elu_done, 1)

            act.wait_ge(gexp_in, 1)
            nc.scalar.activation(z_exp[:, :], z_masked[:, :], ACT.Exp).then_inc(gexp_out, 1)
            for part, cols in enumerate(PARTS):
                act.wait_ge(h_psum, part + 1)
                at = 2 if part == 0 else 0
                nc.scalar.activation(h[:, cols], acc[part][0:N, at:at + cols.stop - cols.start], ACT.Copy,
                                     scale=col(RSTD)).then_inc(h_ready, 1)
            for half in range(2):
                act.wait_ge(sums_psum, half + 1)
                nc.scalar.activation(sumsT[:, 4 * half:4 * half + 4, :], sums_banks[half][:, 0:4 * N].rearrange(
                    "p (c n) -> p c n", c=4), ACT.Copy).then_inc(sums_ready, 1)
            act.wait_ge(inv_ready, 1)
            for piece in range(len(PIECES)):
                elu_parts(piece)

        @block.vector
        def _(dve):
            links = [0]

            def link(ins):
                links[0] += 1
                ins.then_inc(dve_chain, 1)
                dve.wait_ge(dve_chain, links[0])

            arrived = [0] * NRAW

            def transpose_tile(tile):
                m, slot, to = matrix_of(tile), tile % NRAW, tile % NWT
                arrived[slot] += 0 if tile < HALVED_LOADS else 128 if m == T_WO else 64
                if arrived[slot]:
                    dve.wait_ge(raw_in[slot], arrived[slot])
                if tile >= NWT:
                    dve.wait_ge(tile_done, tile - NWT + 1)
                for j in range(2):
                    if tile < HALVED_LOADS:
                        dve.wait_ge(first_in[tile][j], 64)
                    if m in BANDED_OUT:
                        i = raw[:, slot, :].rearrange("p (A j i) -> p j A i", j=2, i=256)[:, j]
                        o = wt[:, to, :].rearrange("p (k j A b) -> p j A k b", k=KC, j=2, b=32)[:, j]
                    else:
                        i = raw[:, slot, :].rearrange("p (j c i) -> p j c i", j=2, i=256)[:, j]
                        o = wt[:, to, :].rearrange("p (k j c b) -> p j c k b", k=KC, j=2, b=32)[:, j]
                    nc.vector.transpose(o, i).then_inc(wt_ready, 1)

            def compare_keys(g):
                dve.wait_ge(keys_psum, g + 1)
                if g:
                    dve.wait_ge(keys_compared, g)
                for j in range(EG):
                    c = EG * g + j
                    last = nc.vector.scalar_tensor_tensor(
                        out=junk[0:EP, j * EP:(j + 1) * EP], in0=misc[g % 4][0:EP, j * EP:(j + 1) * EP],
                        scalar=edge_work[:, 0, c:c + 1], in1=later[:, :], op0=ALU.is_equal, op1=ALU.mult,
                        accum_out=edge_work[:, 1, c:c + 1])
                last.then_inc(keys_compared, 1)

            def read_latest(g):
                dve.wait_ge(latest_psum, g + 1)
                nc.vector.tensor_reduce(latest_g[:, g, :], misc[g % 4][0:N, 0:EG * N].rearrange(
                    "p (c n) -> p n c", c=EG), AX.X, ALU.max).then_inc(latest_read, 1)

            def build_mask():
                dve.wait_ge(latest_read, EC // EG)
                link(nc.vector.tensor_reduce(latest[:, :], latest_g[:, :, :].rearrange("p g n -> p n g"),
                                             AX.X, ALU.max))
                link(nc.vector.tensor_tensor(latest[:, :], latest[:, :], diag3[:, :], ALU.max))
                link(nc.vector.tensor_copy(latest_i[:, :], latest[:, :]))
                link(nc.vector.tensor_single_scalar(latest_i[:, :], latest_i[:, :], 3, op=ALU.bitwise_and))
                link(nc.vector.tensor_copy(mask_part[:, :], latest_i[:, :]))
                dve.wait_ge(etw_ln, 1)
                nc.vector.scalar_tensor_tensor(out=etw_soft[:, :], in0=etw_all[:, :], scalar=0.0,
                                               in1=etw_a[:, :], op0=ALU.max, op1=ALU.add)
                link(nc.vector.tensor_scalar(mask[:, :], latest[:, :], 2.5, NEG, ALU.is_lt, ALU.mult))
                for w in range(4):
                    link(nc.vector.tensor_scalar(weight_term[:, :], mask_part[:, :], float(w),
                                                 etw_soft[:, w:w + 1], ALU.is_equal, ALU.mult))
                    ins = nc.vector.tensor_tensor(mask[:, :], mask[:, :], weight_term[:, :], ALU.add)
                    if w < 3:
                        link(ins)
                    else:
                        ins.then_inc(mask_ready, 1)

            def mask_scores(b):
                dve.wait_ge(scores_psum, b + 1)
                for hh in HEADS_OF[b]:
                    s = slot_of(hh)
                    last = nc.vector.scalar_tensor_tensor(
                        out=probs[:, hh, :], in0=misc[b][0:N, s * N:(s + 1) * N], scalar=SCALE,
                        in1=mask[:, :], op0=ALU.mult, op1=ALU.add)
                link(last)
                heads = probs[:, HEADS_OF[b][0]:HEADS_OF[b][-1] + 1:2, :]
                nc.vector.tensor_reduce(col(NMAX + 4 * b, 4), heads, AX.X, ALU.max, negate=True
                                        ).then_inc(masked_ready, 1)

            def statistics(parts):
                count = 0
                for part in parts:
                    ins = nc.vector.bn_stats(col(STAT + 6 * count, 6), part)
                    count += 1
                link(ins)
                link(nc.vector.bn_aggr(col(AGG, 2), small[0:N, STAT:STAT + 6 * count]))
                nc.vector.tensor_scalar(col(VEPS), col(AGG + 1), EPS, None, ALU.add).then_inc(var_ready, 1)

            dve.wait_ge(x_in, 16)
            nc.vector.tensor_copy(x_band[:, :].rearrange("p (k a d) -> p a k d", k=KC, a=4),
                                  x_nodes[:, :].rearrange("p (a k d) -> p a k d", k=KC, a=4)
                                  ).then_inc(x_band_ready, 1)
            transpose_tile(0)

            def products_with_a(ks):
                for k in ks:
                    dve.wait_ge(gat_w_in[k // 2], 64)
                    if k:
                        dve.wait_ge(wa_ready, k)
                    nc.vector.scalar_tensor_tensor(
                        out=junk[:, :], in0=w_cols[:, k, :], scalar=1.0, in1=gat_a_all[:, 0, :],
                        op0=ALU.mult, op1=ALU.mult, accum_out=wa[:, k, 0:1]).then_inc(wa_ready, 1)

            def divide_mix(g):
                dve.wait_ge(mix_psum, g + 1)
                to = mixed[:, g * HALF:(g + 1) * HALF].rearrange("p (e f a d) -> p e a f d", e=2, f=2, a=4)
                heads = acc[g][0:N, :].rearrange("p (a e f d) -> p e a f d", a=4, e=2, f=2)
                inv = col(ROWINV + 8 * g, 8).rearrange("p (a e f d) -> p e a f d", a=4, e=2, f=1)
                for e in range(2):
                    nc.vector.tensor_tensor(to[:, e], heads[:, e], inv[:, e].to_broadcast([N, 4, 2, 32]),
                                            ALU.mult).then_inc(mixed_ready, 1)

            def evacuate_oT(g):
                dve.wait_ge(oT_psum, g + 1)
                nc.vector.tensor_tensor(
                    oT[:, 4 * g:4 * g + 4, :], misc[g][:, 0:4 * N].rearrange("p (c n) -> p c n", c=4),
                    biasT[:, 6 * KC + 4 * g:6 * KC + 4 * g + 4].rearrange("p (c n) -> p c n", n=1)
                    .to_broadcast([P, 4, N]), ALU.add).then_inc(oT_ready, 1)

            def residual_1(b):
                dve.wait_ge(tile_done, T_WO + 2 * b + 2)
                for i in range(4):
                    chunk = 4 * (i % 2) + 2 * b + i // 2
                    nc.vector.scalar_tensor_tensor(
                        out=yT[:, chunk, :], in0=misc[2 + b][:, i * N:(i + 1) * N],
                        scalar=biasT[:, 3 * KC + chunk:3 * KC + chunk + 1], in1=xT[:, chunk, :],
                        op0=ALU.add, op1=ALU.add).then_inc(yT_ready, 1)

            def edge_columns():
                dve.wait_ge(etw_in, 16)
                nc.vector.scalar_tensor_tensor(out=etw_a[:, :], in0=etw_all[:, :], scalar=-1.0,
                                               in1=etw_all[:, :], op0=ALU.mult, op1=ALU.min).then_inc(etw_pre, 1)
                dve.wait_ge(edge_psum, 1)
                nc.vector.tensor_copy(edge_cols[:, :, :], misc[3][0:EP, 0:3 * EC].rearrange(
                    "p (k c) -> p k c", k=3)).then_inc(edge_cols_ready, 1)
                dve.wait_ge(edge_cols_ready, 1)
                dve.wait_ge(pool_const, 1)
                nc.vector.scalar_tensor_tensor(out=edge_work[:, 0, :], in0=edge_cols[:, 0, :], scalar=float(N),
                                               in1=edge_cols[:, 1, :], op0=ALU.mult, op1=ALU.add)
                link(nc.vector.tensor_scalar(edge_work[:, 2, :], edge_cols[:, 2, :], 0.0, 4.0, ALU.is_equal,
                                             ALU.mult))
                link(nc.vector.tensor_tensor(edge_work[:, 2, :], edge_work[:, 2, :], edge_cols[:, 2, :], ALU.add))
                link(nc.vector.tensor_tensor(edge_work[:, 3, :], edge_work[:, 2, :], chunk_base[:, :], ALU.add))

            for tile in range(1, TILES):
                transpose_tile(tile)
                if tile == T_WO + 1:
                    dve.wait_ge(probs_ready, HEADS)
                    link(nc.vector.reciprocal(col(ROWINV, HEADS), col(ROWSUM, HEADS)))
                    dve.wait_ge(gat_a_in, 16)
                    products_with_a((0,))
                    divide_mix(0)
                    evacuate_oT(0)
                if tile == 2:
                    edge_columns()
                    dve.wait_ge(xT_ready, 2)
                if 5 <= tile < 9:
                    compare_keys(2 * (tile - 5))
                if 5 <= tile < 8:
                    compare_keys(2 * (tile - 5) + 1)
                if tile == 9:
                    compare_keys(7)
                    dve.wait_ge(keys_compared, EC // EG)
                    nc.vector.scalar_tensor_tensor(out=edge_work[:, 4, :], in0=edge_work[:, 1, :],
                                                   scalar=0.5, in1=edge_work[:, 3, :], op0=ALU.is_lt,
                                                   op1=ALU.mult).then_inc(kept_ready, 1)
                if 15 <= tile < 19:
                    read_latest(2 * (tile - 15))
                    read_latest(2 * (tile - 15) + 1)
                if tile == 18:
                    dve.wait_ge(count_psum, 1)
                    nc.vector.tensor_copy(countT[:, :], wide[0][0:N, 0:N]).then_inc(count_ready, 1)
                    dve.wait_ge(count_ready, 1)
                    nc.vector.tensor_scalar(absentT[:, :], countT[:, :], 0.5, NEG, ALU.is_lt, ALU.mult)
                    build_mask()
                    dve.wait_ge(mask_ready, 1)
                if tile == T_WIV:
                    for b in range(4):
                        mask_scores(b)
            products_with_a((1, 2))
            divide_mix(1)
            products_with_a((3,))
            evacuate_oT(1)
            products_with_a((4, 5, 6, 7))
            residual_1(0)
            residual_1(1)
            dve.wait_ge(wa_ready, KC)
            dve.wait_ge(wa1_ready, KC)
            nc.vector.tensor_reduce(wa_sum[:, :], wa.rearrange("p k a -> p a k"), AX.X, ALU.add
                                    ).then_inc(wa_sum_ready, 1)

            dve.wait_ge(y_psum, 2)
            statistics(wide[half][0:N, :] for half in range(2))
            nc.vector.tensor_scalar(col(NEGM), col(AGG), -1.0, None, ALU.mult).then_inc(neg_mean_ready, 1)
            dve.wait_ge(dots_psum, 1)
            nc.vector.tensor_copy(logit_parts[:, 0:2], misc[0][0:N, 0:2])
            link(nc.vector.tensor_copy(logit_parts[:, 2:4], acc[0][0:N, 0:2]))
            dve.wait_ge(neg_mean_ready, 1)
            link(nc.vector.scalar_tensor_tensor(out=col(DOTS, 2), in0=logit_parts[:, 0:2], scalar=col(NEGM),
                                                in1=logit_parts[:, 2:4], op0=ALU.mult, op1=ALU.add))
            dve.wait_ge(rstd_ready, 1)
            nc.vector.tensor_scalar(col(AL, 2), col(DOTS, 2), col(RSTD), None, ALU.mult
                                    ).then_inc(logits_ready, 1)
            def normalise(half):
                nc.vector.tensor_scalar(x1_banded[:, half * HALF:(half + 1) * HALF], wide[half][0:N, :],
                                        col(AGG), col(RSTD), ALU.subtract, ALU.mult).then_inc(x1_ready, 1)

            normalise(0)
            dve.wait_ge(logits_ready, 1)
            dve.wait_ge(spread_psum, 1)
            link(nc.vector.tensor_scalar(z_sum[:, :], misc[2][0:N, 0:N], col(AL + 1), None, ALU.add))
            link(nc.vector.scalar_tensor_tensor(out=z_leaky[:, :], in0=z_sum[:, :], scalar=0.1,
                                                in1=z_sum[:, :], op0=ALU.mult, op1=ALU.max))
            nc.vector.scalar_tensor_tensor(out=z_masked[:, :], in0=z_leaky[:, :], scalar=-1.0, in1=absentT[:, :],
                                           op0=ALU.mult, op1=ALU.add).then_inc(gexp_in, 1)
            dve.wait_ge(gexp_out, 1)
            nc.vector.tensor_tensor(attention[:, :], z_exp[:, :], countT[:, :], ALU.mult).then_inc(adj_ready, 1)
            normalise(1)
            dve.wait_ge(x1_ready, 2)
            nc.vector.tensor_copy(x1[:, :].rearrange("p (a k d) -> p k a d", a=4, k=KC),
                                  x1_banded[:, :].rearrange("p (k a d) -> p k a d", k=KC, a=4)
                                  ).then_inc(x1_back, 1)
            dve.wait_ge(degree_psum, 1)
            link(nc.vector.tensor_scalar(col(INV + 1), misc[1][0:N, 0:1], EPS, None, ALU.add))
            nc.vector.reciprocal(col(INV), col(INV + 1)).then_inc(inv_ready, 1)

            def residual_2():
                for piece, cols in enumerate(PIECES):
                    dve.wait_ge(elu_done, 2 * piece + 1)
                    link(nc.vector.scalar_tensor_tensor(out=y2[:, cols], in0=elu_e[:, cols], scalar=1.0,
                                                        in1=x1[:, cols], op0=ALU.min, op1=ALU.add))
                    dve.wait_ge(elu_done, 2 * piece + 2)
                    link(nc.vector.scalar_tensor_tensor(out=y2[:, cols], in0=elu_r[:, cols], scalar=-1.0,
                                                        in1=y2[:, cols], op0=ALU.add, op1=ALU.add))
                    for c in range(cols.start, cols.stop, P):
                        yield y2[:, c:c + P]

            dve.wait_ge(x1_back, 1)
            statistics(residual_2())
            dve.wait_ge(rstd_ready, 2)
            for half in range(2):
                span = OUT_PARTS[half]
                nc.vector.tensor_scalar(final[:, span], y2[:, span], col(AGG), col(RSTD), ALU.subtract,
                                        ALU.mult).then_inc(final_ready, 1)

        @block.tensor
        def _(pe):
            pe.wait_ge(ident_ready, 1)
            for _ in range(WARM_UP[0]):
                nc.tensor.matmul(misc[3][:, 0:P], ident[:, :], ident[:, :], start=True, stop=True)
            pe.wait_ge(x_band_ready, 1)
            for k in range(KC):
                last = nc.tensor.transpose(misc[k // 4][:, (k % 4) * N:(k % 4 + 1) * N],
                                           x_band[:, k * P:(k + 1) * P], ident[0:N, 0:N])
                if k % 4 == 3:
                    last.then_inc(xT_psum, 1)
            for _ in range(WARM_UP[1]):
                nc.tensor.matmul(misc[3][:, 0:P], ident[:, :], ident[:, :], start=True, stop=True)

            def transpose_biases():
                pe.wait_ge(bias_in, 16 * 7)
                pe.wait_ge(natural_in, 16)
                nc.tensor.transpose(misc[2][:, 0:NB * KC], bias_rows[:, :], ident[0:NB * KC, 0:NB * KC]
                                    ).then_inc(bias_psum, 1)

            def transpose_edges():
                pe.wait_ge(edge_conv, 1)
                for k in range(3):
                    last = nc.tensor.transpose(misc[3][0:EP, k * EC:(k + 1) * EC], edge_rows[0:EC, k, :],
                                               ident[0:EC, 0:EC])
                last.then_inc(edge_psum, 1)

            def column_products(tile, rhs):
                turn = tile
                m, slot = matrix_of(tile), tile % NWT
                if turn >= 2:
                    pe.wait_ge(acc_read, turn - 1)
                for j in range(2):
                    pe.wait_ge(wt_ready, 2 * tile + j + 1)
                    for k in range(KC):
                        if tile == 0 and j == 0 and k % 4 == 0:
                            pe.wait_ge(xT_ready, k // 4 + 1)
                        last = nc.tensor.matmul(acc[turn % 2][:, j * N:(j + 1) * N],
                                                wt[:, slot, k * TR + j * P:k * TR + (j + 1) * P],
                                                rhs[:, k, :], start=(k == 0), stop=(k == KC - 1))
                last.then_inc(tile_done, 1)

            def row_products(tile, part):
                slot, t = tile % NWT, tile % TPM
                pe.wait_ge(wt_ready, 2 * tile + 2)
                order = (0, 4, 1, 5, 2, 6, 3, 7)
                for i in range(4 * part, 4 * part + 4):
                    k = order[i]
                    if tile == T_WIV and i % 2 == 0:
                        pe.wait_ge(acc_read, T_WV + i // 2 + 1)
                    last = nc.tensor.matmul(wide[t // 2][0:N, (t % 2) * TR:(t % 2 + 1) * TR],
                                            vT[:, k, :], wt[:, slot, k * TR:(k + 1) * TR],
                                            start=(i == 0), stop=(i == KC - 1))
                if part == 1:
                    last.then_inc(tile_done, 1)

            def spread_keys(g):
                if g >= 4:
                    pe.wait_ge(keys_compared, g - 3)
                nc.tensor.matmul(misc[g % 4][0:EP, 0:EG * EP], key_weights[:, :],
                                 key_rows[:, g * EG * EP:(g + 1) * EG * EP],
                                 start=True, stop=True).then_inc(keys_psum, 1)

            def latest_edges(g):
                if g >= 4:
                    pe.wait_ge(latest_read, g - 3)
                for j in range(EG):
                    last = nc.tensor.matmul(misc[g % 4][0:N, j * N:(j + 1) * N], src_hot[:, EG * g + j, :],
                                            dst_val[:, EG * g + j, :], start=True, stop=True)
                last.then_inc(latest_psum, 1)

            sources = {T_WQ: xT, T_WK: xT, T_WIQ: qT, T_WIK: kT, T_WV: xT}
            for tile in range(T_WIV):
                if tile == T_WIQ:
                    pe.wait_ge(acc_read, T_WK)
                if tile == T_WIK:
                    pe.wait_ge(acc_read, T_WIQ)
                column_products(tile, sources[matrix_of(tile)])
                if tile == 0:
                    transpose_biases()
                if tile == 1:
                    transpose_edges()
                if tile == 3:
                    pe.wait_ge(keys_placed, 1)
                    pe.wait_ge(edge_cols_ready, 1)
                    pe.wait_ge(bias_ready, 1)
                if 3 <= tile < 7:
                    spread_keys(2 * (tile - 3))
                    spread_keys(2 * (tile - 3) + 1)
                if tile == 12:
                    pe.wait_ge(val_ready, 1)
                    pe.wait_ge(hot_ready, 2)
                    pe.wait_ge(keys_compared, EC // EG)
                if 12 <= tile < 16:
                    latest_edges(2 * (tile - 12))
                    latest_edges(2 * (tile - 12) + 1)
                if tile == 13:
                    for c in range(EC):
                        last = nc.tensor.matmul(wide[0][0:N, 0:N], dst_hot[:, c, :], src_hot[:, c, :],
                                                start=(c == 0), stop=(c == EC - 1))
                    last.then_inc(count_psum, 1)
                if tile == T_WV + 1:
                    pe.wait_ge(acc_read, T_WV)
                    pe.wait_ge(latest_read, EC // EG)
                    for b in range(4):
                        for hh in HEADS_OF[b]:
                            rows = slice(HD * (hh % 2), HD * (hh % 2) + HD)
                            last = nc.tensor.matmul(misc[b][0:N, slot_of(hh) * N:(slot_of(hh) + 1) * N],
                                                    q2T[rows, hh // 2, :], k2T[rows, hh // 2, :],
                                                    start=True, stop=True)
                        last.then_inc(scores_psum, 1)
            pe.wait_ge(count_ready, 1)

            def mix_heads(g):
                pe.wait_ge(wide_read, g + 1)
                for hh in range(8 * g, 8 * g + 8):
                    last = nc.tensor.matmul(acc[g][0:N, (hh % 8) * HD:(hh % 8 + 1) * HD],
                                            probsT[:, 4 * bank_of(hh) + slot_of(hh), :],
                                            v2[:, hh * HD:(hh + 1) * HD], start=True, stop=True)
                last.then_inc(mix_psum, 1)

            def transpose_mixed(g):
                pe.wait_ge(mixed_ready, 2 * g + 2)
                for k in range(4):
                    last = nc.tensor.transpose(misc[g][:, k * N:(k + 1) * N],
                                               mixed[:, (4 * g + k) * P:(4 * g + k + 1) * P],
                                               ident[0:N, 0:N])
                last.then_inc(oT_psum, 1)

            def project(t, g, js):
                tile = T_WO + t
                if g == 0:
                    pe.wait_ge(wt_ready, 2 * tile + 2)
                for j in js:
                    i = 2 * (t % 2) + j
                    for k in range(4 * g, 4 * g + 4):
                        at = k * TR + j * P
                        last = nc.tensor.matmul(misc[2 + t // 2][:, i * N:(i + 1) * N],
                                                wt[:, tile % NWT, at:at + P], oT[:, k, :],
                                                start=(i == 0 and k == 0), stop=(k == KC - 1),
                                                skip_group_check=True)
                if g == 1:
                    last.then_inc(tile_done, 1)

            for tile in (T_WIV, T_WIV + 1):
                row_products(tile, 0)
                row_products(tile, 1)
            pe.wait_ge(masked_ready, 4)
            for b in range(4):
                for hh in HEADS_OF[b]:
                    pe.wait_ge(probs_ready, HEAD_ORDER.index(hh) + 1)
                    last = nc.tensor.transpose(misc[b][0:N, slot_of(hh) * N:(slot_of(hh) + 1) * N],
                                               probs[:, hh, :], ident[0:N, 0:N])
                last.then_inc(probsT_psum, 1)
            row_products(T_WIV + 2, 0)
            row_products(T_WIV + 2, 1)
            pe.wait_ge(probsT_ready, 4)
            mix_heads(0)
            row_products(T_WIV + 3, 0)
            transpose_mixed(0)
            row_products(T_WIV + 3, 1)
            pe.wait_ge(oT_ready, 1)
            project(0, 0, (0, 1))
            mix_heads(1)
            project(1, 0, (0, 1))
            project(2, 0, (0, 1))
            project(3, 0, (0,))
            transpose_mixed(1)
            project(3, 0, (1,))
            pe.wait_ge(oT_ready, 2)
            for t in range(TPM):
                project(t, 1, (0, 1))

            def graph_products(part, ks):
                cols = slice(0, TR) if part == 0 else slice(TR, 2 + PIECES[0].stop)
                for k in ks:
                    last = nc.tensor.matmul(acc[part][0:N, 0:cols.stop - cols.start], yT[:, k, :],
                                            gat_w_sb[:, k, cols], start=(k == 0), stop=(k == KC - 1))
                return last

            def subtract_mean(part):
                at = 2 if part == 0 else 0
                cols = PARTS[part]
                nc.tensor.matmul(acc[part][0:N, at:at + cols.stop - cols.start], mean_rows[:, :],
                                 wsum[:, cols], start=False, stop=True, skip_group_check=True
                                 ).then_inc(h_psum, 1)

            def sum_neighbours(half):
                pe.wait_ge(x1_ready, half + 1)
                for k in range(4):
                    c = (4 * half + k) * P
                    last = nc.tensor.matmul(sums_banks[half][:, k * N:(k + 1) * N], x1_banded[:, c:c + P],
                                            attention[:, :], start=True, stop=True)
                last.then_inc(sums_psum, 1)

            def summed_products(piece):
                for k in range(KC):
                    if piece == 1 and k % 4 == 0:
                        pe.wait_ge(sums_ready, k // 4 + 1)
                    last = nc.tensor.matmul(z_banks[piece][0:N, 0:width(piece)], sumsT[:, k, :],
                                            w_cols[:, k, PIECES[piece]], start=(k == 0), stop=(k == KC - 1))
                last.then_inc(agg_psum, 1)

            for g in range(4):
                pe.wait_ge(gat_w_in[g], 64)
            pe.wait_ge(yT_ready, 4)
            pe.wait_ge(wa_ready, KC)
            pe.wait_ge(wa1_ready, 6)
            graph_products(0, (0, 4, 1, 5))
            pe.wait_ge(yT_ready, 8)
            for k in range(KC):
                last = nc.tensor.transpose(wide[k // 4][0:N, (k % 4) * P:(k % 4 + 1) * P], yT[:, k, :],
                                           ident[:, :])
                if k % 4 == 3:
                    last.then_inc(y_psum, 1)
            pe.wait_ge(wa_sum_ready, 1)
            nc.tensor.matmul(misc[0][0:N, 0:2], ones[:, :], wa_sum[:, :], start=True, stop=True)
            graph_products(0, (2, 6, 3, 7)).then_inc(dots_psum, 1)
            graph_products(1, (0, 4, 1, 5, 2))
            pe.wait_ge(logits_ready, 1)
            nc.tensor.matmul(misc[2][0:N, 0:N], col(AL).to_broadcast([N, N]), ident[0:N, 0:N],
                             start=True, stop=True).then_inc(spread_psum, 1)
            pe.wait_ge(neg_mean_ready, 1)
            nc.tensor.matmul(misc[1][:, 0:N], col(NEGM).to_broadcast([N, P]), ident[0:N, 0:N],
                             start=True, stop=True).then_inc(mean_psum, 1)
            graph_products(1, (6, 3, 7))
            pe.wait_ge(mean_rows_ready, 1)
            pe.wait_ge(wsum_ready, 1)
            subtract_mean(0)
            subtract_mean(1)
            pe.wait_ge(adj_ready, 1)
            nc.tensor.matmul(misc[1][0:N, 0:1], attention[:, :], ones[0:N, 0:1], start=True, stop=True
                             ).then_inc(degree_psum, 1)
            sum_neighbours(0)
            sum_neighbours(1)
            pe.wait_ge(h_ready, 2)
            nc.tensor.matmul(wide[0][0:N, 0:width(0)], attention[:, :], h[:, PIECES[0]],
                             start=True, stop=True).then_inc(agg_psum, 1)
            for piece in (1, 2, 3):
                summed_products(piece)


_INS = ['x', 'src', 'dst', 'edge_type_5', 'L0_gnn_edge_type_weights', 'L0_gnn_wq', 'L0_gnn_bq', 'L0_gnn_wk',
        'L0_gnn_bk', 'L0_gnn_wv', 'L0_gnn_bv', 'L0_gnn_wiq', 'L0_gnn_biq', 'L0_gnn_wik', 'L0_gnn_bik',
        'L0_gnn_wiv', 'L0_gnn_biv', 'L0_gnn_wo', 'L0_gnn_bo', 'L1_gnn_W', 'L1_gnn_a']


def kernel(**inputs):
    import numpy as _np
    import concourse.bacc as _bacc
    from concourse import mybir as _mybir
    from concourse.bass_utils import run_bass_kernel_spmd as _run

    nc = _bacc.Bacc("TRN2", target_bir_lowering=False, num_devices=1)
    arrays, args = {}, []
    for name in _INS:
        a = _np.ascontiguousarray(inputs[name])
        arrays[f"in_{name}"] = a
        args.append(nc.dram_tensor(f"in_{name}", a.shape, _mybir.dt.from_np(a.dtype), kind="ExternalInput").ap())
    out = nc.dram_tensor("out_0", (96, 1024), _mybir.dt.float32, kind="ExternalOutput").ap()
    build(nc, *args, out)
    r = _run(nc, [arrays], core_ids=[0])
    return r.results[0]["out_0"]
```
